# Optimizing a Trainium2 kernel written in Bass

```python
import numpy as np
import jax
import jax.numpy as jnp

def _softmax(x, axis=-1):
    return jax.nn.softmax(x, axis=axis)

def _gelu(x):
    return jax.nn.gelu(x, approximate=True)

def _silu(x):
    return jax.nn.silu(x)

def _sigmoid(x):
    return jax.nn.sigmoid(x)

def _layernorm(x, axis=-1, eps=1e-05):
    m = jnp.mean(x, axis=axis, keepdims=True)
    v = jnp.var(x, axis=axis, keepdims=True)
    return (x - m) / jnp.sqrt(v + eps)

def _scatter_add(tgt, idx, src, axis=0):
    return tgt.at[idx].add(src)

def _segment_sum(src, seg, n):
    return jax.ops.segment_sum(src, seg, n)
kernel_name = 'mk_prb_d1_jaxref_r8_3d9be5'

def setup_inputs(seed: int=0):
    np.random.seed(seed)
    _w = jnp.asarray

    def _L0_attn_setup():
        import jax, jax.numpy as jnp
        import numpy as np
        HEADS = 16
        key = jax.random.key(seed)
        k1, k2, k3, k4 = jax.random.split(key, 4)
        C, T, E = (8, 512, 128)
        D = E // HEADS
        x = jax.random.normal(k1, (C, T, E), dtype=jnp.float32)
        Wq = jax.random.normal(k2, (D, D), dtype=jnp.float32) * (1.0 / np.sqrt(D))
        Wk = jax.random.normal(k3, (D, D), dtype=jnp.float32) * (1.0 / np.sqrt(D))
        Wv = jax.random.normal(k4, (D, D), dtype=jnp.float32) * (1.0 / np.sqrt(D))
        return {'x': x, 'Wq': Wq, 'Wk': Wk, 'Wv': Wv}
    _L0_attn_in = _L0_attn_setup()

    def _L0_ffn_setup():
        import jax, jax.numpy as jnp
        import numpy as np
        DIM = 128
        INTER = 176
        N_EXPERTS = 16
        TOPK = 2
        N_SHARED = 2
        SHARED_INTER = N_SHARED * INTER
        ROUTE_SCALE = 1.0
        key = jax.random.key(seed)
        ks = jax.random.split(key, 16)
        s = 0.02
        return {'x': jax.random.normal(ks[0], (2, 256, DIM), dtype=jnp.float32), 'gate_w': jax.random.normal(ks[1], (DIM, N_EXPERTS), dtype=jnp.float32) * s, 'gate_b': jnp.zeros((N_EXPERTS,), dtype=jnp.float32), 'w1': jax.random.normal(ks[2], (N_EXPERTS, DIM, INTER), dtype=jnp.float32) * s, 'b1': jnp.zeros((N_EXPERTS, INTER), dtype=jnp.float32), 'w3': jax.random.normal(ks[3], (N_EXPERTS, DIM, INTER), dtype=jnp.float32) * s, 'b3': jnp.zeros((N_EXPERTS, INTER), dtype=jnp.float32), 'w2': jax.random.normal(ks[4], (N_EXPERTS, INTER, DIM), dtype=jnp.float32) * s, 'b2': jnp.zeros((N_EXPERTS, DIM), dtype=jnp.float32), 'sw1': jax.random.normal(ks[5], (DIM, SHARED_INTER), dtype=jnp.float32) * s, 'sb1': jax.random.normal(ks[6], (SHARED_INTER,), dtype=jnp.float32) * s, 'sw3': jax.random.normal(ks[7], (DIM, SHARED_INTER), dtype=jnp.float32) * s, 'sb3': jax.random.normal(ks[8], (SHARED_INTER,), dtype=jnp.float32) * s, 'sw2': jax.random.normal(ks[9], (SHARED_INTER, DIM), dtype=jnp.float32) * s, 'sb2': jax.random.normal(ks[10], (DIM,), dtype=jnp.float32) * s}
    _L0_ffn_in = _L0_ffn_setup()
    _d = {'L0_attn_x': _L0_attn_in['x'], 'L0_attn_Wq': _L0_attn_in['Wq'], 'L0_attn_Wk': _L0_attn_in['Wk'], 'L0_attn_Wv': _L0_attn_in['Wv'], 'L0_ffn_gate_w': _L0_ffn_in['gate_w'], 'L0_ffn_gate_b': _L0_ffn_in['gate_b'], 'L0_ffn_w1': _L0_ffn_in['w1'], 'L0_ffn_b1': _L0_ffn_in['b1'], 'L0_ffn_w3': _L0_ffn_in['w3'], 'L0_ffn_b3': _L0_ffn_in['b3'], 'L0_ffn_w2': _L0_ffn_in['w2'], 'L0_ffn_b2': _L0_ffn_in['b2'], 'L0_ffn_sw1': _L0_ffn_in['sw1'], 'L0_ffn_sb1': _L0_ffn_in['sb1'], 'L0_ffn_sw3': _L0_ffn_in['sw3'], 'L0_ffn_sb3': _L0_ffn_in['sb3'], 'L0_ffn_sw2': _L0_ffn_in['sw2'], 'L0_ffn_sb2': _L0_ffn_in['sb2']}
    _x0 = _d['L0_attn_x']
    _d['L0_attn_x'] = jax.random.normal(jax.random.fold_in(jax.random.key(seed), 1), (16, 256, 128), dtype=_x0.dtype)
    del _x0
    return _d

def reference(L0_attn_x, L0_attn_Wq, L0_attn_Wk, L0_attn_Wv, L0_ffn_gate_w, L0_ffn_gate_b, L0_ffn_w1, L0_ffn_b1, L0_ffn_w3, L0_ffn_b3, L0_ffn_w2, L0_ffn_b2, L0_ffn_sw1, L0_ffn_sb1, L0_ffn_sw3, L0_ffn_sb3, L0_ffn_sw2, L0_ffn_sb2):

    def _L0_attn_ref(x, Wq, Wk, Wv):
        import jax, jax.numpy as jnp
        import numpy as np
        HEADS = 16
        C, T, E = x.shape
        H = HEADS
        D = E // H
        xr = x.reshape(C, T, H, D)
        q = jnp.einsum('cthd,ed->cthe', xr, Wq)
        k = jnp.einsum('cthd,ed->cthe', xr, Wk)
        v = jnp.einsum('cthd,ed->cthe', xr, Wv)
        diag_scores = jnp.einsum('cthd,cthd->cth', q, k) / jnp.sqrt(jnp.asarray(E, x.dtype))
        probs = jax.nn.softmax(diag_scores, axis=0)
        vsum = v.sum(axis=1)
        attn = probs[..., None] * vsum[:, None, :, :]
        return attn.reshape(C, T, E)

    def _L0_ffn_ref(x, gate_w, gate_b, w1, b1, w3, b3, w2, b2, sw1, sb1, sw3, sb3, sw2, sb2):
        import jax, jax.numpy as jnp
        import numpy as np
        DIM = 128
        INTER = 176
        N_EXPERTS = 16
        TOPK = 2
        N_SHARED = 2
        SHARED_INTER = N_SHARED * INTER
        ROUTE_SCALE = 1.0
        shape = x.shape
        xf = x.reshape(-1, DIM)
        logits = xf @ gate_w + gate_b
        scores = jax.nn.softmax(logits.astype(jnp.float32), axis=-1)
        top_vals, top_idx = jax.lax.top_k(scores, TOPK)
        weights = (top_vals * ROUTE_SCALE).astype(x.dtype)
        cw = (jax.nn.one_hot(top_idx, N_EXPERTS, dtype=x.dtype) * weights[..., None]).sum(axis=1)
        h = jnp.einsum('td,edh->teh', xf, w1) + b1
        g = jnp.einsum('td,edh->teh', xf, w3) + b3
        a = jax.nn.silu(h) * g
        y = jnp.einsum('teh,ehd,te->td', a, w2, cw) + cw @ b2
        z = jax.nn.silu(xf @ sw1 + sb1) * (xf @ sw3 + sb3) @ sw2 + sb2
        return (y + z).reshape(shape)
    x = L0_attn_x
    xn = _layernorm(x, axis=-1)
    x = x + _L0_attn_ref(xn, L0_attn_Wq, L0_attn_Wk, L0_attn_Wv) + _L0_ffn_ref(xn, L0_ffn_gate_w, L0_ffn_gate_b, L0_ffn_w1, L0_ffn_b1, L0_ffn_w3, L0_ffn_b3, L0_ffn_w2, L0_ffn_b2, L0_ffn_sw1, L0_ffn_sb1, L0_ffn_sw3, L0_ffn_sb3, L0_ffn_sw2, L0_ffn_sb2)
    return x

_drawn_inputs = setup_inputs


def setup_inputs(seed=0):
    import zlib

    import numpy as np

    out = dict(_drawn_inputs(seed))
    spreads = {'L0_ffn_gate_b': (0.0, 0.8),
     'L0_ffn_b1': (0.0, 0.8),
     'L0_ffn_b3': (0.0, 0.8),
     'L0_ffn_b2': (0.0, 0.8)}
    factors = {'L0_ffn_gate_w': 7.468,
     'L0_ffn_w1': 8.0,
     'L0_ffn_w3': 8.0,
     'L0_ffn_w2': 8.0,
     'L0_ffn_sw1': 8.0,
     'L0_ffn_sb1': 8.0,
     'L0_ffn_sw3': 8.0,
     'L0_ffn_sb3': 8.0,
     'L0_ffn_sw2': 8.0,
     'L0_ffn_sb2': 18.143}
    for name, (base, spread) in spreads.items():
        noise = np.random.default_rng([zlib.crc32(name.encode()), seed]).standard_normal(out[name].shape)
        drawn = base * np.exp(spread * noise) if base else spread * noise
        out[name] = jnp.asarray(drawn.astype(out[name].dtype))
    for name, factor in factors.items():
        out[name] = (out[name] * factor).astype(out[name].dtype)
    return out
```

```python
import concourse.bass as bass
from concourse import mybir
from contextlib import ExitStack

ALU = mybir.AluOpType
ACT = mybir.ActivationFunctionType
AX = mybir.AxisListType
F32 = mybir.dt.float32
BF16 = mybir.dt.bfloat16
I32 = mybir.dt.int32
U32 = mybir.dt.uint32

P = 128
C, T = 16, 256
N = C * T
NT = N // P
GT = 4
NG = NT // GT
GW = GT * P
H, D = 16, 8
NE, F = 16, 176
FH = F // 2
F2 = 2 * F
SF = 352
SCH = [(0, 128), (128, 128), (256, 96)]
NB = len(SCH)
CT = C // (NG // 2)
NS = 80
UN = 8
ROW = P + 2
YL = 4
EPS = 1e-5
BIG = 3.0e38
NBIAS = NE * (F2 + P) + P

K_ID, K_BLK, K_U, K_ONE = 0, 128, 256, 384
K_BO = 512
K_REV = K_BO + H
K_TILE = K_REV + NE
K_TOK = K_TILE + NS
K_TOK2 = K_TOK + NT
K_PAD = K_TOK2 + NT
K_EPS = K_PAD + NS
KW = K_EPS + 2
NY = 2 * N + NS * P


class Chain:

    def __init__(self, eng, sem):
        self.eng, self.sem, self.base, self.n = eng, sem, 0, 0

    def did(self, ins):
        ins.then_inc(self.sem, 1)
        self.n += 1

    def sync(self, ins=None):
        if ins is not None:
            self.did(ins)
        self.eng.wait_ge(self.sem, self.base + self.n)

    def turn(self, start, it, per):
        self.base, self.n = start + it * per, 0

    def after(self, total):
        self.base, self.n = 0, total


def build(nc, d):
    ctx = ExitStack()
    with ctx:
        def sb(name, shape, dt=F32):
            return ctx.enter_context(nc.sbuf_tensor(name, shape, dt))

        def sem(name):
            return ctx.enter_context(nc.semaphore(name))

        xslot = nc.dram_tensor("xslot", (NS * P, ROW), F32).ap()
        ydram = nc.dram_tensor("ydram", (NY, P), F32).ap()
        bdram = nc.dram_tensor("bdram", (3, NBIAS), BF16).ap()

        kc = sb("kc", [P, KW])
        ubf = sb("ubf", [P, P], BF16)
        obf = sb("obf", [P, P], BF16)
        X = sb("X", [P, NT, P])
        XR = sb("XR", [P, NT, ROW])
        xnT = sb("xnT", [P, N])
        prod = sb("prod", [P, 2, GW])
        st = sb("st", [P, NT, 6])
        mv = sb("mv", [P, 3, NT])
        rstd = sb("rstd", [P, NT])
        xsum = sb("xsum", [P, C])
        wqk = sb("wqk", [P, 3, P])
        wbd = sb("wbd", [P, 3, P])
        mbd = sb("mbd", [P, P])
        gw = sb("gw", [P, NE])
        gb = sb("gb", [P, NE])
        sw1 = sb("sw1", [P, SF])
        sw3 = sb("sw3", [P, SF])
        sw2 = sb("sw2", [P, NB, P])
        sbc = sb("sbc", [P, NB, 2])
        fw = sb("fw", [P, NS * ROW])
        fill = fw[:, :].rearrange("p (s r) -> p s r", r=ROW)
        w13 = fw[:, 0:NE * F2]
        w2 = fw[0:FH, NE * F2:NE * (F2 + 2 * P)]
        braw = sb("braw", [P, NBIAS // P])
        bres = sb("bres", [P, NBIAS // P])
        bprt = sb("bprt", [P, 3, NBIAS // P], BF16)
        bsp = sb("bsp", [3, NBIAS], BF16)
        Vb = sb("Vb", [P, C, P])
        lg = sb("lg", [P, NT, NE])
        ex = sb("ex", [P, NT, NE])
        sd = sb("sd", [P, C, 2 * H])
        pr = sb("pr", [P, C, 2 * H])
        at = sb("at", [P, CT, 2, P])
        alt = sb("alt", [P, NT, 2])
        eq = sb("eq", [P, NT, NE])
        lg2 = sb("lg2", [P, NT, NE])
        m1 = sb("m1", [P, NT, NE])
        m2 = sb("m2", [P, NT, NE])
        mbf = sb("mbf", [P, NT, NE], BF16)
        tj = sb("tj", [P, NE, NT])
        gj = sb("gj", [P, NE, NT])
        one = sb("one", [P, NE * NT])
        slot = sb("slot", [P, NT, NE])
        sm = sb("sm", [P, 8, NT])
        se = sb("se", [P, 8, NE])
        ntl = sb("ntl", [P, NE], I32)
        idx = sb("idx", [P, 2, NT], I32)
        ecmp = sb("ecmp", [1, NS, NE])
        emf = sb("emf", [1, NS])
        emi = sb("emi", [1, NS], I32)
        sS = sb("sS", [P, 2, NB, GW])
        sG = sb("sG", [P, 2, NB, GW])
        Qv = sG[:].rearrange("p b c w -> p (b c w)")[:, 0:C * P].rearrange("p (c e) -> p c e", c=C)
        yl = XR[:].rearrange("p t r -> p (t r)")[:, 0:YL * 2 * GW].rearrange("p (b t k e) -> p b t k e", b=YL, k=2, e=P)
        ob = sS[:].rearrange("p b c w -> p (b c w)")[:, 0:YL * GW].rearrange("p (b w) -> p b w", b=YL)
        RX = sb("RX", [P, UN, ROW])
        meta = sb("meta", [P, UN, 2])
        prod_w = prod[:].rearrange("p b w -> p (b w)")
        rxT = prod_w[:, 0:2 * P].rearrange("p (b w) -> p b w", b=2)
        sg = prod_w[:, 2 * P:2 * P + 2 * F].rearrange("p (b w) -> p b w", b=2)
        ra = prod_w[:, 2 * P + 2 * F:2 * P + 4 * F].rearrange("p (b w) -> p b w", b=2)
        raT = sb("raT", [FH, 2, 2 * P])
        yb = sb("yb", [P, UN, P])

        PS = ctx.enter_context(nc.psum_tensor("PS", [P, 8, 512], F32))
        MX, MX2, R1, R2, SUM, CW1, CW2 = range(7)
        NEX, TLF, PIN, BAS, OFF = range(5)

        ident = kc[:, K_ID:K_ID + P]
        rev_b = kc[:, K_REV:K_REV + NE].rearrange("p (a e) -> p a e", a=1).to_broadcast([P, NT, NE])

        def over_e(col):
            return col.rearrange("p (t a) -> p t a", a=1).to_broadcast([P, NT, NE])

        l_x = [sem(f"l_x{g}") for g in range(NG)]
        x_in = sem("x_in")
        l_kc, l_ws, l_sh, l_w13, l_w2, l_b = (sem(n) for n in ("l_kc", "l_ws", "l_sh", "l_w13", "l_w2", "l_b"))
        cd, ca, cp = sem("cd"), sem("ca"), sem("cp")
        k_bf, k_wbd, k_mbd, k_bprt = sem("k_bf"), sem("k_wbd"), sem("k_mbd"), sem("k_bprt")
        d_bst, d_bld, d_fill = sem("d_bst"), sem("d_bld"), sem("d_fill")
        s_st, s_var, s_std, s_xn, s_tp, s_xt = (sem(n) for n in ("s_st", "s_var", "s_std", "s_xn", "s_tp", "s_xt"))
        s_y, s_pr, s_sc = sem("s_y"), sem("s_pr"), sem("s_sc")
        s_lg, s_dl, s_ds, s_exg, s_exa, s_q, s_v, s_vb = (sem(n) for n in ("s_lg", "s_dl", "s_ds", "s_exg", "s_exa", "s_q", "s_v", "s_vb"))
        s_m, s_rk, s_em, s_idx, s_cw = (sem(n) for n in ("s_m", "s_rk", "s_em", "s_idx", "s_cw"))
        s_up, s_sg, s_sm, s_z, s_za = (sem(n) for n in ("s_up", "s_sg", "s_sm", "s_z", "s_za"))
        s_at, s_ax = sem("s_at"), sem("s_ax")
        d_sc = [[sem(f"d_sc{k}{h}") for h in range(2)] for k in range(2)]
        d_rx = [sem(f"d_rx{u}") for u in range(UN)]
        d_y = [sem(f"d_y{u}") for u in range(UN)]
        r_meta, r_tp, r_xt, r_up, r_sg, r_a, r_at, r_att, r_dn, r_y = (
            sem(n) for n in ("r_meta", "r_tp", "r_xt", "r_up", "r_sg", "r_a", "r_at", "r_att", "r_dn", "r_y"))
        d_yl = [sem(f"d_yl{b}") for b in range(YL)]
        d_o = [sem(f"d_o{b}") for b in range(YL)]
        p_gate = sem("p_gate")
        s_f1, s_f2 = sem("s_f1"), sem("s_f2")

        x_v = d["x"].rearrange("(t p) e -> p t e", p=P)
        out_v = d["out"].rearrange("(t p) e -> p t e", p=P)
        y_v = ydram[0:2 * N, :].rearrange("(p t k) e -> p t k e", t=NT, k=2)
        xs_v = xslot.rearrange("(s p) r -> s p r", p=P)

        def j_turn(j, u, ahead):
            return loop_it[0] + (u + ahead) // UN

        loop_it = [None]

        def steps(eng, run, top=None):
            turns = (NS - 4) // UN
            for j in range(-1, 3 + UN):
                run(j, j, True)
            with eng.Fori(1, turns) as it:
                loop_it[0] = it
                if top:
                    top(it)
                for u in range(3, 3 + UN):
                    run(it * UN + u, u, False)
            for j in range(3 + turns * UN, NS + 4):
                run(j, j, True)

        def has(j, fixed):
            return not fixed or 0 <= j < NS

        block = ctx.enter_context(nc.Block())

        @block.sync
        def _(sp):
            sp.dma_start(braw[:], d["biases"]).then_inc(l_b, 16)
            sp.dma_start(kc[:], d["kc"]).then_inc(l_kc, 16)
            for g in range(NG):
                sp.dma_start(X[:, g * GT:(g + 1) * GT, :], x_v[:, g * GT:(g + 1) * GT, :]).then_inc(l_x[g], 16)
                if g == 0:
                    sp.dma_start(wqk[:].rearrange("p a b -> p (a b)"), d["wqk"]).then_inc(l_ws, 16)
                    sp.dma_start(gw[:], d["gate_w"]).then_inc(l_ws, 16)
                    sp.dma_start(gb[:], d["gate_b"].to_broadcast([P, NE])).then_inc(l_ws, 16)
            sp.dma_start(sw1[:], d["sw1"]).then_inc(l_sh, 16)
            sp.dma_start(sw3[:], d["sw3"]).then_inc(l_sh, 16)
            sp.dma_start(sw2[:, 0:2, :], d["sw2"][0:256, :].rearrange("(c p) n -> p c n", p=P)).then_inc(l_sh, 16)
            sp.dma_start(sw2[0:96, 2, :], d["sw2"][256:SF, :]).then_inc(l_sh, 16)
            sp.dma_start(sbc[:, 0:2, :], d["sb_a"]).then_inc(l_sh, 16)
            sp.dma_start(sbc[0:96, 2:3, :], d["sb_b"]).then_inc(l_sh, 16)
            for g in range(NG):
                sp.wait_ge(l_x[g], 16)
                sp.sem_inc(x_in, 1)
            sp.wait_ge(d_fill, 16)
            sp.dma_start(w13, d["w13"]).then_inc(l_w13, 16)
            sp.dma_start(w2, d["w2"]).then_inc(l_w2, 16)
            for k in range(2):
                for h in range(2):
                    sp.wait_ge(d_sc[k][h], 16 * (NT // 2))

            def load(j, u, turn):
                if turn is not None:
                    sp.wait_ge(r_tp, j - UN + 1)
                    sp.wait_ge(r_meta, j - UN + 1)
                sp.dma_start(RX[:, u, :], xs_v[j]).then_inc(d_rx[u], 16)

            for u in range(UN):
                load(u, u, None)
            with sp.Fori(0, NS // UN - 1) as it:
                for u in range(UN):
                    load((it + 1) * UN + u, u, it)
            for u in range(UN):
                sp.wait_ge(d_y[u], 16 * (NS // UN))

            def fetch(g, b):
                sp.dma_start(yl[:, b], y_v[:, bass.ds(g * GT, GT), :, :]).then_inc(d_yl[b], 16)

            for b in range(YL):
                fetch(b, b)
            with sp.Fori(0, NG // YL - 1) as it:
                for b in range(YL):
                    sp.wait_ge(s_f2, it * YL + b + 1)
                    fetch(it * YL + YL + b, b)
            for b in range(YL):
                sp.wait_ge(d_o[b], 16 * (NG // YL))

        @block.gpsimd
        def _(pool):
            ch = Chain(pool, cp)

            def gate():
                pool.sem_inc(p_gate, 1)

            pool.memset(one[:], 1.0)
            ch.did(pool.memset(fw[:, :], 0.0))
            pool.wait_ge(l_kc, 16)
            ch.sync()
            ch.did(pool.tensor_copy(fill[:, :, P:P + 1].bitcast(I32),
                                    kc[:, K_PAD:K_PAD + NS].bitcast(I32).rearrange("p (s a) -> p s a", a=1)))
            ch.did(pool.tensor_copy(XR[:, :, P:P + 1].bitcast(I32),
                                    kc[:, K_TOK:K_TOK + NT].bitcast(I32).rearrange("p (s a) -> p s a", a=1)))
            ch.sync()
            pool.dma_start(xslot.rearrange("(p s) r -> p (s r)", p=P),
                           fw[:, :]).then_inc(d_fill, 16)
            ch.did(pool.tensor_copy(alt[:, :, 0:1].bitcast(I32),
                                    kc[:, K_TOK2:K_TOK2 + NT].bitcast(I32).rearrange("p (s a) -> p s a", a=1)))
            pool.wait_ge(s_xt, 2 * NG)
            pool.wait_ge(k_wbd, 1)
            pool.tensor_tensor(Qv, xsum[:].rearrange("p (c a) -> p c a", a=1).to_broadcast([P, C, P]),
                               wbd[:, 2:3, :].to_broadcast([P, C, P]), ALU.mult).then_inc(s_q, 1)
            pool.wait_ge(d_fill, 16)
            pool.wait_ge(s_idx, 2)
            pool.wait_ge(s_cw, 2)
            for k in range(2):
                for h in range(2):
                    half = slice(h * NT // 2, (h + 1) * NT // 2)
                    if k == 1:
                        pool.wait_ge(d_sc[0][h], 16 * (NT // 2))
                        ch.sync(pool.tensor_copy(XR[:, half, P:ROW], alt[:, half, :]))
                    for t in range(half.start, half.stop):
                        pool.indirect_dma_start(xslot, bass.IndirectOffsetOnAxis(ap=idx[:, k, t:t + 1], axis=0),
                                                XR[:, t, :], None).then_inc(d_sc[k][h], 16)

            def run(j, u, fixed):
                if has(j + 1, fixed):
                    v = (u + 1) % UN
                    turn = (j + 1) // UN if fixed else None
                    pool.wait_ge(d_rx[v], 16 * (turn + 1) if fixed else j_turn(j, u, 1) * 16 + 16)
                    pool.wait_ge(d_y[v], 16 * turn if fixed else j_turn(j, u, 1) * 16)
                    gate()
                    pool.tensor_copy(meta[:, v, :], RX[:, v, P:ROW]).then_inc(r_meta, 1)
                if has(j - 3, fixed):
                    v = (u - 3) % UN
                    pool.wait_ge(r_y, j - 2)
                    pool.wait_ge(r_meta, j - 2)
                    gate()
                    pool.indirect_dma_start(ydram, bass.IndirectOffsetOnAxis(ap=meta[:, v, 0:1].bitcast(I32), axis=0),
                                            yb[:, v, :], None).then_inc(d_y[v], 16)

            steps(pool, run)
        @block.vector
        def _(dve):
            ch = Chain(dve, cd)
            dve.wait_ge(l_b, 16)
            ch.sync(dve.tensor_copy(bprt[:, 0, :], braw[:]))
            ch.sync(dve.tensor_tensor(bres[:], braw[:], bprt[:, 0, :], ALU.subtract))
            ch.sync(dve.tensor_copy(bprt[:, 1, :], bres[:]))
            ch.sync(dve.tensor_tensor(bres[:], bres[:], bprt[:, 1, :], ALU.subtract))
            dve.tensor_copy(bprt[:, 2, :], bres[:]).then_inc(k_bprt, 1)
            dve.wait_ge(l_kc, 16)
            dve.tensor_copy(ubf[:], kc[:, K_U:K_U + P])
            dve.tensor_copy(obf[:], kc[:, K_ONE:K_ONE + P]).then_inc(k_bf, 1)
            with dve.Fori(0, NG) as g:
                dve.wait_ge(x_in, g + 1)
                for t in range(GT):
                    ins = dve.bn_stats(st[:, bass.ds(g * GT + t, 1), :].rearrange("p a s -> p (a s)"),
                                       X[:, bass.ds(g * GT + t, 1), :].rearrange("p a s -> p (a s)"))
                ins.then_inc(s_st, 1)
            dve.wait_ge(s_st, NG)
            me, mo, ve, vo = (st[:, :, k] for k in (1, 4, 2, 5))
            mean, var, dm = mv[:, 0, :], mv[:, 1, :], mv[:, 2, :]
            ch.did(dve.tensor_tensor(dm, me, mo, ALU.subtract))
            ch.did(dve.tensor_tensor(mean, me, mo, ALU.add))
            ch.sync(dve.tensor_tensor(var, ve, vo, ALU.add))
            ch.did(dve.tensor_tensor(dm, dm, dm, ALU.mult))
            ch.did(dve.tensor_scalar(mean, mean, 0.5, None, ALU.mult))
            ch.sync(dve.tensor_scalar(var, var, 1.0 / P, None, ALU.mult))
            dve.scalar_tensor_tensor(out=var, in0=dm, scalar=0.25, in1=var, op0=ALU.mult, op1=ALU.add).then_inc(s_var, 1)
            dve.wait_ge(l_ws, 48)
            dve.tensor_tensor(wbd[:], wqk[:], kc[:, K_BLK:K_BLK + P].rearrange("p (a b) -> p a b", a=1)
                              .to_broadcast([P, 3, P]), ALU.mult).then_inc(k_wbd, 1)
            dve.wait_ge(s_std, 1)
            ch.sync(dve.reciprocal(rstd[:], rstd[:]))

            def norm(g):
                for t in range(g * GT, (g + 1) * GT):
                    ins = dve.tensor_scalar(XR[:, t, 0:P], X[:, t, :], mean[:, t:t + 1], rstd[:, t:t + 1],
                                            ALU.subtract, ALU.mult)
                ins.then_inc(s_xn, 1)

            norm(0)
            norm(1)
            for g in range(NG):
                if g + 2 < NG:
                    norm(g + 2)
                dve.wait_ge(s_y, g + 1)
                if g >= 2:
                    dve.wait_ge(s_sc, g - 1)
                dve.tensor_tensor(prod[:, g % 2, :], PS[:, 2 + g % 2, :], xnT[:, g * GW:(g + 1) * GW],
                                  ALU.mult).then_inc(s_pr, 1)

            dve.wait_ge(s_sc, NG)
            psL = PS[:, 4, :].rearrange("p (t e) -> p t e", e=NE)
            psS = PS[:, 5, :].rearrange("p (c r) -> p c r", c=C)
            dve.tensor_tensor(lg[:], psL, gb[:].rearrange("p (a e) -> p a e", a=1).to_broadcast([P, NT, NE]),
                              ALU.add).then_inc(s_lg, 1)
            mxa = se[:, 6:8, :].rearrange("p a e -> p (a e)")
            ch.did(dve.tensor_reduce(mxa, psS.rearrange("p c r -> p r c"), AX.X, ALU.max))
            dve.wait_ge(s_lg, 1)
            ch.sync(dve.tensor_reduce(sm[:, MX, :], lg[:], AX.X, ALU.max))
            dve.tensor_tensor(ex[:], lg[:], over_e(sm[:, MX, :]), ALU.subtract).then_inc(s_dl, 1)
            dve.tensor_tensor(sd[:], psS, mxa.rearrange("p (a r) -> p a r", a=1).to_broadcast([P, C, 2 * H]),
                              ALU.subtract).then_inc(s_ds, 1)

            def pick(logits, mx, r, m):
                ch.sync(dve.tensor_tensor(eq[:], logits[:], over_e(sm[:, mx, :]), ALU.is_equal))
                ch.sync(dve.tensor_tensor(eq[:], eq[:], rev_b, ALU.mult))
                ch.sync(dve.tensor_reduce(sm[:, r, :], eq[:], AX.X, ALU.max))
                ch.sync(dve.tensor_tensor(m[:], over_e(sm[:, r, :]), rev_b, ALU.is_equal))

            pick(lg, MX, R1, m1)
            ch.sync(dve.scalar_tensor_tensor(out=lg2[:].rearrange("p t e -> p (t e)"), in0=m1[:].rearrange("p t e -> p (t e)"),
                                             scalar=-BIG, in1=lg[:].rearrange("p t e -> p (t e)"), op0=ALU.mult, op1=ALU.add))
            ch.sync(dve.tensor_reduce(sm[:, MX2, :], lg2[:], AX.X, ALU.max))
            pick(lg2, MX2, R2, m2)
            dve.tensor_tensor(mbf[:], m1[:], m2[:], ALU.add).then_inc(s_m, 1)

            dve.wait_ge(s_exg, 1)
            ch.did(dve.tensor_reduce(sm[:, SUM, :], ex[:], AX.X, ALU.add))
            ch.sync(dve.tensor_tensor(eq[:], ex[:], m2[:], ALU.mult))
            ch.did(dve.tensor_reduce(sm[:, CW2, :], eq[:], AX.X, ALU.add))
            ch.sync(dve.reciprocal(sm[:, CW1, :], sm[:, SUM, :]))
            ch.did(dve.tensor_tensor(sm[:, CW2, :], sm[:, CW2, :], sm[:, CW1, :], ALU.mult))
            dve.tensor_copy(XR[:, :, P + 1:P + 2], sm[:, CW1, :].rearrange("p (t a) -> p t a", a=1)).then_inc(s_cw, 1)
            ch.sync()
            dve.tensor_copy(alt[:, :, 1:2], sm[:, CW2, :].rearrange("p (t a) -> p t a", a=1)).then_inc(s_cw, 1)

            dve.wait_ge(s_rk, 1)
            ch.sync(dve.tensor_copy(tj[:], PS[:, 7, :].rearrange("p (t e) -> p e t", e=NE)))
            tjf, gjf = tj[:].rearrange("p e t -> p (e t)"), gj[:].rearrange("p e t -> p (e t)")
            ch.did(dve.tensor_tensor_scan(gjf, one[:], tjf, 0.0, ALU.mult, ALU.add))
            ch.sync(dve.tensor_reduce(se[:, NEX, :], tj[:], AX.X, ALU.add))
            ch.did(dve.tensor_tensor(gj[:], gj[:], tj[:], ALU.subtract))
            ch.sync(dve.tensor_scalar(ntl[:], se[:, NEX, :], 127.0, None, ALU.add))
            ch.sync(dve.tensor_scalar(ntl[:], ntl[:], 7, None, ALU.arith_shift_right))
            ch.sync(dve.tensor_copy(se[:, TLF, :], ntl[:]))
            ch.sync(dve.tensor_tensor_scan(se[:, PIN, :], one[:, 0:NE], se[:, TLF, :], 0.0, ALU.mult, ALU.add))
            ch.sync(dve.tensor_tensor(se[:, BAS, :], se[:, PIN, :], se[:, TLF, :], ALU.subtract))
            ch.sync(dve.scalar_tensor_tensor(out=se[:, OFF, :], in0=se[:, BAS, :], scalar=float(P),
                                             in1=gj[:, :, 0], op0=ALU.mult, op1=ALU.subtract))
            ch.sync(dve.tensor_tensor(slot[:], gj[:].rearrange("p e t -> p t e"),
                                      se[:, OFF:OFF + 1, :].to_broadcast([P, NT, NE]), ALU.add))
            ch.sync(dve.tensor_tensor(slot[:], slot[:], PS[:, 6, :].rearrange("p (t e) -> p t e", e=NE), ALU.add))
            ch.did(dve.tensor_tensor(eq[:], slot[:], m1[:], ALU.mult))
            ch.sync(dve.tensor_tensor(lg2[:], slot[:], m2[:], ALU.mult))
            ch.did(dve.tensor_reduce(sm[:, R1, :], eq[:], AX.X, ALU.add))
            ch.sync(dve.tensor_reduce(sm[:, R2, :], lg2[:], AX.X, ALU.add))
            dve.tensor_copy(idx[:, 0, :], sm[:, R1, :]).then_inc(s_idx, 1)
            dve.tensor_copy(idx[:, 1, :], sm[:, R2, :]).then_inc(s_idx, 1)
            ch.sync(dve.tensor_tensor(
                ecmp[:], kc[0:1, K_TILE:K_TILE + NS].rearrange("p (s a) -> p s a", a=1).to_broadcast([1, NS, NE]),
                se[0:1, PIN:PIN + 1, :].to_broadcast([1, NS, NE]), ALU.is_ge))
            ch.sync(dve.tensor_reduce(emf[:], ecmp[:], AX.X, ALU.add))
            dve.tensor_scalar(emi[:], emf[:], float(NE - 1), None, ALU.min).then_inc(s_em, 1)

            def gated(g, b):
                for c, (_, m) in enumerate(SCH):
                    dve.wait_ge(s_sg, 2 * (g * NB + c) + 2)
                    dve.tensor_tensor(sS[0:m, b, c, :], sS[0:m, b, c, :], sG[0:m, b, c, :], ALU.mult).then_inc(s_sm, 1)

            def add_z(g, b):
                dve.wait_ge(s_z, g + 1)
                v = X[:, bass.ds(g * GT, GT), :].rearrange("p t e -> p (t e)")
                dve.tensor_tensor(v, PS[:, 4 + b, :], v, ALU.add).then_inc(s_za, 1)

            def attend(part):
                for k in range(CT):
                    c = part * CT + k
                    prv = pr[:, bass.ds(c, 1), :].rearrange("p a (b h) -> p (a b) h", b=2).rearrange(
                        "p b (h a) -> p b h a", a=1).to_broadcast([P, 2, H, D])
                    vbv = Vb[:, bass.ds(c, 1), :].rearrange("p a (h e) -> p a h e", h=H).to_broadcast([P, 2, H, D])
                    ins = dve.tensor_tensor(at[:, k].rearrange("p b (h e) -> p b h e", h=H), prv, vbv, ALU.mult)
                ins.then_inc(s_at, 1)
                dve.wait_ge(s_at, part + 1)
                xv = X[:, bass.ds(part * CT * 2, CT * 2), :].rearrange("p t e -> p (t e)")
                dve.tensor_tensor(xv, xv, at[:].rearrange("p k b e -> p (k b e)"), ALU.add).then_inc(s_ax, 1)

            gated(0, 0)
            gated(1, 1)
            dve.wait_ge(s_exa, 1)
            asum = se[:, 6:8, :].rearrange("p a e -> p (a e)")
            ch.sync(dve.tensor_reduce(asum, pr[:].rearrange("p c r -> p r c"), AX.X, ALU.add))
            ch.sync(dve.reciprocal(asum, asum))
            ch.sync(dve.tensor_tensor(pr[:], pr[:], asum.rearrange("p (a r) -> p a r", a=1).to_broadcast([P, C, 2 * H]), ALU.mult))
            dve.wait_ge(s_vb, C // GT)
            attend(0)
            dve.wait_ge(s_ax, 1)
            add_z(0, 0)
            add_z(1, 1)
            with dve.Fori(1, NG // 2) as it:
                for b in range(2):
                    gated(it * 2 + b, b)
                attend(it)
                dve.wait_ge(s_ax, it + 1)
                for b in range(2):
                    add_z(it * 2 + b, b)

            def run(j, u, fixed):
                if has(j - 0, fixed):
                    b = u % 2
                    dve.wait_ge(r_sg, j + 1)
                    dve.wait_ge(r_at, max(j - 1, 0) if fixed else j - 1)
                    dve.tensor_tensor(ra[:, b, :], sg[:, b, :], PS[:, 2 + b, F:F2], ALU.mult).then_inc(r_a, 1)
                if has(j - 2, fixed):
                    b, v = u % 2, (u - 2) % UN
                    dve.wait_ge(r_dn, j - 1)
                    dve.wait_ge(r_meta, j - 1)
                    if not fixed:
                        dve.wait_ge(d_y[v], j_turn(j, u, -2) * 16)
                    elif j - 2 >= UN:
                        dve.wait_ge(d_y[v], 16 * ((j - 2) // UN))
                    dve.tensor_scalar(yb[:, v, :], PS[:, 6 + b, 0:P], meta[:, v, 1:2], None, ALU.mult).then_inc(r_y, 1)

            steps(dve, run)
            def close(g, b, it, first):
                dve.wait_ge(d_yl[b], it * 16 + 16)
                if not first:
                    dve.wait_ge(d_o[b], it * 16)
                o = ob[:, b].rearrange("p (t e) -> p t e", t=GT)
                dve.tensor_tensor(o, yl[:, b, :, 0, :], X[:, bass.ds(g * GT, GT), :], ALU.add).then_inc(s_f1, 1)
                dve.wait_ge(s_f1, g + 1)
                dve.tensor_tensor(o, o, yl[:, b, :, 1, :], ALU.add).then_inc(s_f2, 1)

            for b in range(YL):
                close(b, b, 0, True)
            with dve.Fori(1, NG // YL) as it:
                for b in range(YL):
                    close(it * YL + b, b, it, False)

        @block.scalar
        def _(act):
            act.wait_ge(k_bprt, 1)
            for k in range(3):
                act.dma_start(bdram[k].rearrange("(p w) -> p w", p=P), bprt[:, k, :]).then_inc(d_bst, 16)
            act.wait_ge(d_bst, 48)
            act.dma_start(bsp[:], bdram).then_inc(d_bld, 16)
            act.wait_ge(s_var, 1)
            act.wait_ge(l_kc, 16)
            act.activation(rstd[:], mv[:, 1, :], ACT.Sqrt,
                           bias=kc[:, K_EPS:K_EPS + 1]).then_inc(s_std, 1)
            act.wait_ge(k_mbd, 1)
            act.activation(mbd[:], PS[:, 6, 0:P], ACT.Copy).then_inc(k_mbd, 1)

            for g in range(NG):
                act.wait_ge(s_tp, g + 1)
                for k in range(2):
                    act.activation(xnT[:, g * GW + k * T:g * GW + (k + 1) * T], PS[:, g % 2, k * T:(k + 1) * T],
                                   ACT.Copy, accum_out=xsum[:, 2 * g + k:2 * g + k + 1]).then_inc(s_xt, 1)
            act.wait_ge(s_dl, 1)
            act.activation(ex[:].rearrange("p t e -> p (t e)"), ex[:].rearrange("p t e -> p (t e)"), ACT.Exp).then_inc(s_exg, 1)
            act.wait_ge(s_ds, 1)
            act.activation(pr[:].rearrange("p c r -> p (c r)"), sd[:].rearrange("p c r -> p (c r)"), ACT.Exp,
                           scale=float(P) ** -0.5).then_inc(s_exa, 1)
            for q, bank in enumerate((6, 7, 4, 5)):
                act.wait_ge(s_v, q + 1)
                act.activation(Vb[:, GT * q:GT * q + GT, :].rearrange("p c e -> p (c e)"), PS[:, bank, :],
                               ACT.Copy).then_inc(s_vb, 1)

            def gates(g, b, first):
                for c, (_, m) in enumerate(SCH):
                    k = c % 2 if b == 0 else (c + 1) % 2
                    act.wait_ge(s_up, g * NB + c + 1)
                    if not first:
                        act.wait_ge(s_z, g - 1)
                    act.activation(sS[0:m, b, c, :], PS[0:m, k, :], ACT.Silu, bias=sbc[0:m, c, 0:1]).then_inc(s_sg, 1)
                    act.activation(sG[0:m, b, c, :], PS[0:m, 2 + k, :], ACT.Identity, bias=sbc[0:m, c, 1:2]).then_inc(s_sg, 1)

            act.wait_ge(l_sh, 96)
            gates(0, 0, True)
            gates(1, 1, True)
            with act.Fori(1, NG // 2) as it:
                for b in range(2):
                    gates(it * 2 + b, b, False)

            def run(j, u, fixed):
                if has(j + 1, fixed):
                    b = (u + 1) % 2
                    act.wait_ge(r_tp, j + 2)
                    act.wait_ge(r_up, max(j, 0) if fixed else j)
                    act.activation(rxT[:, b, :], PS[:, b, 0:P], ACT.Copy).then_inc(r_xt, 1)
                if has(j, fixed):
                    b = u % 2
                    act.wait_ge(r_up, j + 1)
                    act.wait_ge(r_a, max(j - 1, 0) if fixed else j - 1)
                    act.activation(sg[:, b, :], PS[:, 2 + b, 0:F], ACT.Silu).then_inc(r_sg, 1)
                if has(j - 1, fixed):
                    b = (u - 1) % 2
                    act.wait_ge(r_at, j)
                    act.wait_ge(r_dn, max(j - 2, 0) if fixed else j - 2)
                    act.activation(raT[:, b, :], PS[0:FH, 4 + b, 0:2 * P], ACT.Copy).then_inc(r_att, 1)

            steps(act, run)
            with act.Fori(0, NG // YL) as it:
                for b in range(YL):
                    g = it * YL + b
                    act.wait_ge(s_f2, g + 1)
                    act.dma_start(out_v[:, bass.ds(g * GT, GT), :], ob[:, b, :].rearrange("p (t e) -> p t e", t=GT)).then_inc(d_o[b], 16)

        @block.tensor
        def _(pe):
            pe.wait_ge(k_wbd, 1)
            pe.matmul(PS[:, 6, 0:P], wbd[:, 0, :], wbd[:, 1, :], start=True, stop=True).then_inc(k_mbd, 1)
            pe.wait_ge(l_ws, 48)
            pe.wait_ge(k_mbd, 2)

            def turn(g):
                pe.wait_ge(s_xn, g + 1)
                if g >= 2:
                    pe.wait_ge(s_xt, 2 * g - 2)
                for t in range(GT):
                    ins = pe.transpose(PS[:, g % 2, t * P:(t + 1) * P], XR[:, g * GT + t, 0:P], ident)
                ins.then_inc(s_tp, 1)

            def project(g):
                pe.wait_ge(s_xt, 2 * g + 2)
                if g >= 2:
                    pe.wait_ge(s_pr, g - 1)
                pe.matmul(PS[:, 2 + g % 2, :], mbd[:], xnT[:, g * GW:(g + 1) * GW], start=True, stop=True).then_inc(s_y, 1)
                for t in range(g * GT, (g + 1) * GT):
                    pe.matmul(PS[:, 4, t * NE:(t + 1) * NE], xnT[:, t * P:(t + 1) * P], gw[:], start=True, stop=True)

            def scores(g):
                pe.wait_ge(s_pr, g + 1)
                for t in range(GT):
                    ins = pe.matmul(PS[:, 5, (g * GT + t) * H:(g * GT + t + 1) * H], prod[:, g % 2, t * P:(t + 1) * P],
                                    kc[:, K_BO:K_BO + H], start=True, stop=True)
                ins.then_inc(s_sc, 1)

            turn(0)
            turn(1)
            for g in range(NG):
                project(g)
                if g + 2 < NG:
                    turn(g + 2)
                if g >= 1:
                    scores(g - 1)
            scores(NG - 1)

            pe.wait_ge(s_q, 1)
            for q, bank in enumerate((6, 7, 4, 5)):
                if bank == 4:
                    pe.wait_ge(s_lg, 1)
                    pe.wait_ge(s_ds, 1)
                pe.matmul(PS[:, bank, :], kc[:, K_ONE:K_ONE + P], Qv[:, GT * q:GT * q + GT, :].rearrange("p c e -> p (c e)"),
                          start=True, stop=True).then_inc(s_v, 1)

            def up(g, b, first):
                for c, (f, m) in enumerate(SCH):
                    k = c % 2 if b == 0 else (c + 1) % 2
                    n = g * NB + c
                    if not (first and b == 0 and c < 2):
                        pe.wait_ge(s_sg, 2 * n - 2)
                    xv = xnT[:, bass.ds(g * GW, GW)]
                    pe.matmul(PS[0:m, k, :], sw1[:, f:f + m], xv, start=True, stop=True)
                    pe.matmul(PS[0:m, 2 + k, :], sw3[:, f:f + m], xv, start=True, stop=True).then_inc(s_up, 1)

            def down(g, b, first):
                pe.wait_ge(s_sm, g * NB + NB)
                if not first:
                    pe.wait_ge(s_za, g - 1)
                for t in range(GT):
                    zt = PS[:, 4 + b, t * P:(t + 1) * P]
                    pe.matmul(zt, obf[0:3, :], bsp[:, NBIAS - P:NBIAS], start=True, stop=False)
                    for c, (_, m) in enumerate(SCH):
                        ins = pe.matmul(zt, sS[0:m, b, c, t * P:(t + 1) * P], sw2[0:m, c, :], start=False, stop=(c == NB - 1))
                ins.then_inc(s_z, 1)

            pe.wait_ge(l_sh, 96)
            up(0, 0, True)
            up(1, 1, True)
            pe.wait_ge(k_bf, 1)
            pe.wait_ge(s_m, 1)
            pe.wait_ge(s_vb, C // GT)
            mk = mbf[:].rearrange("p t e -> p (t e)")
            pe.matmul(PS[:, 6, :], ubf[:], mk, start=True, stop=True)
            pe.matmul(PS[:, 7, :], obf[:], mk, start=True, stop=True).then_inc(s_rk, 1)
            pe.wait_ge(d_bld, 16)
            down(0, 0, True)
            down(1, 1, True)
            with pe.Fori(1, NG // 2) as it:
                for b in range(2):
                    up(it * 2 + b, b, False)
                for b in range(2):
                    down(it * 2 + b, b, False)

            pe.wait_ge(l_w13, 16)
            pe.wait_ge(l_w2, 16)
            pe.wait_ge(s_em, 1)
            pe.wait_ge(s_sg, 2 * NG * NB)
            pe.wait_ge(s_za, NG)

            held = [pe.alloc_register(f"expert{v}") for v in range(UN)]

            def read_expert(j, u):
                at = slice(j, j + 1) if isinstance(j, int) else bass.ds(j, 1)
                pe.reg_load(held[u % UN], emi[0:1, at])

            def expert(u):
                return pe.snap(held[u % UN], min_val=0, max_val=NE - 1)

            def run(j, u, fixed):
                if has(j + 1, fixed):
                    b, v = (u + 1) % 2, (u + 1) % UN
                    pe.wait_ge(d_rx[v], 16 * ((j + 1) // UN + 1) if fixed else j_turn(j, u, 1) * 16 + 16)
                    pe.wait_ge(r_xt, max(j, 0) if fixed else j)
                    pe.transpose(PS[:, b, 0:P], RX[:, v, 0:P], ident).then_inc(r_tp, 1)
                if has(j, fixed):
                    b = u % 2
                    e = expert(u)
                    pe.wait_ge(r_xt, j + 1)
                    pe.wait_ge(r_a, max(j - 1, 0) if fixed else j - 1)
                    pe.matmul(PS[:, 2 + b, 0:F2], obf[0:3, :], bsp[:, bass.ds(e * F2, F2)], start=True, stop=False)
                    pe.matmul(PS[:, 2 + b, 0:F2], rxT[:, b, :], w13[:, bass.ds(e * F2, F2)], start=False,
                              stop=True).then_inc(r_up, 1)
                    if has(j + 1, fixed):
                        read_expert(j + 1, u + 1)
                if has(j - 1, fixed):
                    b = (u - 1) % 2
                    pe.wait_ge(r_a, j)
                    pe.wait_ge(r_att, max(j - 2, 0) if fixed else j - 2)
                    pe.transpose(PS[0:FH, 4 + b, 0:P], ra[:, b, 0:FH], ident)
                    pe.transpose(PS[0:FH, 4 + b, P:2 * P], ra[:, b, FH:F], ident).then_inc(r_at, 1)
                if has(j - 2, fixed):
                    b = u % 2
                    e = expert(u - 2)
                    pe.wait_ge(r_att, j - 1)
                    pe.wait_ge(r_y, max(j - 3, 0) if fixed else j - 3)
                    pe.matmul(PS[:, 6 + b, 0:P], obf[0:3, :], bsp[:, bass.ds(e * P + NE * F2, P)], start=True, stop=False)
                    for k in range(2):
                        ins = pe.matmul(PS[:, 6 + b, 0:P], raT[:, b, k * P:(k + 1) * P],
                                        w2[:, bass.ds(e * 2 * P + k * P, P)], start=False, stop=(k == 1))
                    ins.then_inc(r_dn, 1)

            read_expert(0, 0)
            steps(pe, run)


def constants():
    import numpy as np
    k = np.zeros((P, KW), np.float32)
    i, j = np.arange(P)[:, None], np.arange(P)[None, :]
    k[:, K_ID:K_ID + P] = i == j
    k[:, K_BLK:K_BLK + P] = i // D == j // D
    k[:, K_U:K_U + P] = i < j
    k[:, K_ONE:K_ONE + P] = 1
    k[:, K_BO:K_BO + H] = i // D == np.arange(H)[None, :]
    k[:, K_REV:K_REV + NE] = NE - np.arange(NE)
    k[:, K_TILE:K_TILE + NS] = np.arange(NS)
    kb = k.view(np.int32)
    kb[:, K_TOK:K_TOK + NT] = (i * NT + np.arange(NT)[None, :]) * 2
    kb[:, K_TOK2:K_TOK2 + NT] = kb[:, K_TOK:K_TOK + NT] + 1
    kb[:, K_PAD:K_PAD + NS] = 2 * N + i * NS + np.arange(NS)[None, :]
    k[:, K_EPS] = EPS
    return k


def arrays_of(inp):
    import numpy as np
    a = {n: np.asarray(v) for n, v in inp.items()}
    f = "L0_ffn_"
    w13 = np.concatenate([a[f + "w1"], a[f + "w3"]], axis=2)
    b13 = np.concatenate([a[f + "b1"], a[f + "b3"]], axis=1)
    r = {
        "x": a["L0_attn_x"].reshape(N, P),
        "kc": constants(),
        "wqk": np.concatenate([np.tile(a["L0_attn_Wq"], (H, H)), np.tile(a["L0_attn_Wk"], (H, H)),
                               np.tile(a["L0_attn_Wv"].T, (H, H))], axis=1),
        "gate_w": a[f + "gate_w"], "gate_b": a[f + "gate_b"].reshape(1, NE),
        "biases": np.concatenate([b13.reshape(-1), a[f + "b2"].reshape(-1), a[f + "sb2"]]).reshape(P, NBIAS // P),
        "sw1": a[f + "sw1"], "sw3": a[f + "sw3"], "sw2": a[f + "sw2"],
        "sb_a": np.stack([a[f + "sb1"][:256].reshape(2, P).T, a[f + "sb3"][:256].reshape(2, P).T], axis=2),
        "sb_b": np.stack([a[f + "sb1"][256:], a[f + "sb3"][256:]], axis=1)[:, None, :],
        "w13": w13.transpose(1, 0, 2).reshape(P, NE * F2),
        "w2": a[f + "w2"].reshape(NE, 2, FH, P).transpose(2, 0, 1, 3).reshape(FH, NE * 2 * P),
    }
    return {n: np.ascontiguousarray(v) for n, v in r.items()}


def program(nc, arrays):
    d = {n: nc.dram_tensor(f"in_{n}", v.shape, mybir.dt.from_np(v.dtype), kind="ExternalInput").ap()
         for n, v in arrays.items()}
    d["out"] = nc.dram_tensor("out_0", (N, P), F32, kind="ExternalOutput").ap()
    build(nc, d)


def kernel(**inputs):
    import concourse.bacc as bacc
    from concourse.bass_utils import run_bass_kernel_spmd
    arrays = arrays_of(inputs)
    nc = bacc.Bacc("TRN2", target_bir_lowering=False, num_devices=1)
    program(nc, arrays)
    r = run_bass_kernel_spmd(nc, [{f"in_{n}": v for n, v in arrays.items()}], core_ids=[0])
    return r.results[0]["out_0"].reshape(C, T, P)
```

```python
import concourse.bass as bass
from concourse import mybir
from contextlib import ExitStack

ALU = mybir.AluOpType
ACT = mybir.ActivationFunctionType
AX = mybir.AxisListType
F32 = mybir.dt.float32
BF16 = mybir.dt.bfloat16
I32 = mybir.dt.int32
U32 = mybir.dt.uint32

P = 128
C, T = 16, 256
N = C * T
NT = N // P
GT = 4
NG = NT // GT
GW = GT * P
NQ = NG // 2
QT = 2 * GT
NPOOL = 1
HT = NT // 2
H, D = 16, 8
NE, F = 16, 176
FH = F // 2
F2 = 2 * F
SF = 352
SCH = [(0, 128), (128, 128), (256, 96)]
NB = len(SCH)
CT = C // (NG // 2)
NS = 80
UN = 8
ROW = P + 2
YL = 4
G_BANK = (4, 7)
EPS = 1e-5
BIG = 3.0e38
NBIAS = NE * (F2 + P) + P

K_ID, K_BLK, K_U, K_ONE = 0, 128, 256, 384
K_REV = 512
K_TILE = K_REV + NE
K_TOK = K_TILE + NS
K_TOK2 = K_TOK + NT
K_PAD = K_TOK2 + NT
K_EPS = K_PAD + NS
KW = K_EPS + 2
NY = 2 * N + NS * P


class Chain:

    def __init__(self, eng, sem):
        self.eng, self.sem, self.base, self.n = eng, sem, 0, 0

    def did(self, ins):
        ins.then_inc(self.sem, 1)
        self.n += 1

    def sync(self, ins=None):
        if ins is not None:
            self.did(ins)
        self.eng.wait_ge(self.sem, self.base + self.n)

    def turn(self, start, it, per):
        self.base, self.n = start + it * per, 0

    def after(self, total):
        self.base, self.n = 0, total


def build(nc, d):
    ctx = ExitStack()
    with ctx:
        def sb(name, shape, dt=F32):
            return ctx.enter_context(nc.sbuf_tensor(name, shape, dt))

        def sem(name):
            return ctx.enter_context(nc.semaphore(name))

        xslot = nc.dram_tensor("xslot", (NS * P, ROW), F32).ap()
        ydram = nc.dram_tensor("ydram", (NY, P), F32).ap()
        bdram = nc.dram_tensor("bdram", (3, NBIAS), BF16).ap()

        kc = sb("kc", [P, KW])
        lbf = sb("lbf", [P, P], BF16)
        obf = sb("obf", [P, P], BF16)
        X = sb("X", [P, NT, P])
        XR = sb("XR", [P, NT, ROW])
        xnT = sb("xnT", [P, N])
        prod = sb("prod", [P, 2, GW])
        st = sb("st", [P, NT, 6])
        mv = sb("mv", [P, NT, 2])
        rstd = sb("rstd", [P, NT])
        xsum = sb("xsum", [P, C])
        wqk = sb("wqk", [P, 3, P])
        wbd = sb("wbd", [P, 3, P])
        mbd = sb("mbd", [P, P])
        gw = sb("gw", [P, NE])
        gb = sb("gb", [P, NE])
        sw1 = sb("sw1", [P, SF])
        sw3 = sb("sw3", [P, SF])
        sw2 = sb("sw2", [P, NB, P])
        sbc = sb("sbc", [P, NB, 2])
        fw = sb("fw", [P, NS * ROW])
        fill = fw[:, :].rearrange("p (s r) -> p s r", r=ROW)
        w13 = fw[:, 0:NE * F2]
        w2 = fw[0:FH, NE * F2:NE * (F2 + 2 * P)]
        braw = sb("braw", [P, NBIAS // P])
        bres = sb("bres", [P, NBIAS // P])
        bprt = sb("bprt", [P, 3, NBIAS // P], BF16)
        bsp = sb("bsp", [3, NBIAS], BF16)
        Vb = sb("Vb", [P, C, P])
        lg = sb("lg", [P, NT, NE])
        ex = sb("ex", [P, NT, NE])
        sc = sb("sc", [P, NT * H])
        sd = sb("sd", [P, C, 2 * H])
        pr = sb("pr", [P, C, 2 * H])
        at = sb("at", [P, CT, 2, P])
        alt = sb("alt", [P, NT, 2])
        eq = sb("eq", [P, NT, NE])
        lg2 = sb("lg2", [P, NT, NE])
        m1 = sb("m1", [P, NT, NE])
        m2 = sb("m2", [P, NT, NE])
        mbf = sb("mbf", [P, NE, NT], BF16)
        cum = sb("cum", [P, NE, NT], BF16)
        keep = sb("keep", [P, NE, NT])
        slot = sb("slot", [P, NT, NE])
        sm = sb("sm", [P, 8, NT])
        se = sb("se", [P, 8, NE])
        ntl = sb("ntl", [P, NE], I32)
        idx = sb("idx", [P, 2, NT], I32)
        emf = sb("emf", [1, NS])
        emi = sb("emi", [1, NS], I32)
        sS = sb("sS", [P, 2, NB, GW])
        sG = sb("sG", [P, 2, NB, GW])
        ecmp = sb("ecmp", [1, NS, NE])
        Qv = sb("Qv", [P, C, P])
        yl = XR[:].rearrange("p t r -> p (t r)")[:, 0:YL * 2 * GW].rearrange("p (b t k e) -> p b t k e", b=YL, k=2, e=P)
        ob = sS[:].rearrange("p b c w -> p (b c w)")[:, 0:YL * GW].rearrange("p (b w) -> p b w", b=YL)
        RX = sb("RX", [P, UN, ROW])
        meta = sb("meta", [P, UN, 2])
        prod_w = prod[:].rearrange("p b w -> p (b w)")
        rxT = prod_w[:, 0:2 * P].rearrange("p (b w) -> p b w", b=2)
        sg = prod_w[:, 2 * P:2 * P + 2 * F].rearrange("p (b w) -> p b w", b=2)
        ra = prod_w[:, 2 * P + 2 * F:2 * P + 4 * F].rearrange("p (b w) -> p b w", b=2)
        Qv_w = Qv[:].rearrange("p c e -> p (c e)")
        yb = Qv_w[:, 0:UN * P].rearrange("p (u e) -> p u e", e=P)
        raT = Qv_w[0:FH, UN * P:(UN + 4) * P].rearrange("p (b w) -> p b w", b=2)

        PS = ctx.enter_context(nc.psum_tensor("PS", [P, 8, 512], F32))
        MX, MX2, R1, R2, SUM, CW1, CW2 = range(7)
        NEX, TLF, PIN, BAS, OFF = range(5)

        ident = kc[:, K_ID:K_ID + P]
        rev_b = kc[:, K_REV:K_REV + NE].rearrange("p (a e) -> p a e", a=1).to_broadcast([P, HT, NE])

        def over_e(col):
            return col.rearrange("p (t a) -> p t a", a=1).to_broadcast([P, HT, NE])

        def norm_tiles(g, mine):
            cut = (g + 1) * GT - (NPOOL if g >= 2 else 0)
            return range(cut, (g + 1) * GT) if mine else range(g * GT, cut)

        l_x = [sem(f"l_x{g}") for g in range(NG // 2)]
        l_kc, l_ws, l_sh, l_w13, l_w2, l_b = (sem(n) for n in ("l_kc", "l_ws", "l_sh", "l_w13", "l_w2", "l_b"))
        cd, ca, cp = sem("cd"), sem("ca"), sem("cp")
        k_bf, k_wbd, k_mbd, k_bprt, k_keep = (sem(n) for n in ("k_bf", "k_wbd", "k_mbd", "k_bprt", "k_keep"))
        d_bst, d_bld, d_fill = sem("d_bst"), sem("d_bld"), sem("d_fill")
        s_var, s_std, s_rs, s_xn, s_xp, s_tp, s_xt = (sem(n) for n in ("s_var", "s_std", "s_rs", "s_xn", "s_xp", "s_tp", "s_xt"))
        s_gl, s_y, s_pr = (sem(n) for n in ("s_gl", "s_y", "s_pr"))
        s_lg, s_dl, s_ds, s_exg, s_exa, s_q, s_v, s_vb = (sem(n) for n in ("s_lg", "s_dl", "s_ds", "s_exg", "s_exa", "s_q", "s_v", "s_vb"))
        s_cum, s_tot, s_rk, s_em, s_idx, s_cw = (sem(n) for n in ("s_cum", "s_tot", "s_rk", "s_em", "s_idx", "s_cw"))
        s_up, s_sg, s_sm, s_z, s_za = (sem(n) for n in ("s_up", "s_sg", "s_sm", "s_z", "s_za"))
        s_at, s_ax = sem("s_at"), sem("s_ax")
        d_sc = [[sem(f"d_sc{k}{h}") for h in range(2)] for k in range(2)]
        d_rx = [sem(f"d_rx{u}") for u in range(UN)]
        d_y = [sem(f"d_y{u}") for u in range(UN)]
        r_meta, r_tp, r_xt, r_up, r_sg, r_a, r_at, r_att, r_dn, r_y = (
            sem(n) for n in ("r_meta", "r_tp", "r_xt", "r_up", "r_sg", "r_a", "r_at", "r_att", "r_dn", "r_y"))
        d_yl = [sem(f"d_yl{b}") for b in range(YL)]
        d_o = [sem(f"d_o{b}") for b in range(YL)]
        p_gate = sem("p_gate")
        s_f1, s_f2 = sem("s_f1"), sem("s_f2")

        x_v = d["x"].rearrange("(t p) e -> p t e", p=P)
        out_v = d["out"].rearrange("(t p) e -> p t e", p=P)
        y_v = ydram[0:2 * N, :].rearrange("(p t k) e -> p t k e", t=NT, k=2)
        xs_v = xslot.rearrange("(s p) r -> s p r", p=P)

        def j_turn(j, u, ahead):
            return loop_it[0] + (u + ahead) // UN

        loop_it = [None]

        def steps(eng, run, top=None):
            turns = (NS - 4) // UN
            for j in range(-1, 3 + UN):
                run(j, j, True)
            with eng.Fori(1, turns) as it:
                loop_it[0] = it
                if top:
                    top(it)
                for u in range(3, 3 + UN):
                    run(it * UN + u, u, False)
            for j in range(3 + turns * UN, NS + 4):
                run(j, j, True)

        def has(j, fixed):
            return not fixed or 0 <= j < NS

        block = ctx.enter_context(nc.Block())

        @block.sync
        def _(sp):
            for g in range(NQ):
                two = slice(g * QT, (g + 1) * QT)
                sp.dma_start(X[:, two, :], x_v[:, two, :]).then_inc(l_x[g], 16)
            sp.wait_ge(d_fill, 16)
            sp.dma_start(w13, d["w13"]).then_inc(l_w13, 16)
            sp.dma_start(w2, d["w2"]).then_inc(l_w2, 16)
            for k in range(2):
                for h in range(2):
                    sp.wait_ge(d_sc[k][h], 16 * (NT // 2))

            def load(j, u, turn):
                if turn is not None:
                    sp.wait_ge(r_tp, j - UN + 1)
                    sp.wait_ge(r_meta, j - UN + 1)
                sp.dma_start(RX[:, u, :], xs_v[j]).then_inc(d_rx[u], 16)

            for u in range(UN):
                load(u, u, None)
            with sp.Fori(0, NS // UN - 1) as it:
                for u in range(UN):
                    load((it + 1) * UN + u, u, it)
            for u in range(UN):
                sp.wait_ge(d_y[u], 16 * (NS // UN))

            def fetch(g, b):
                sp.dma_start(yl[:, b], y_v[:, bass.ds(g * GT, GT), :, :]).then_inc(d_yl[b], 16)

            for b in range(YL):
                fetch(b, b)
            with sp.Fori(0, NG // YL - 1) as it:
                for b in range(YL):
                    sp.wait_ge(s_f2, it * YL + b + 1)
                    fetch(it * YL + YL + b, b)
            for b in range(YL):
                sp.wait_ge(d_o[b], 16 * (NG // YL))

        @block.gpsimd
        def _(pool):
            ch = Chain(pool, cp)

            def gate():
                pool.sem_inc(p_gate, 1)

            pool.memset(keep[:], 1.0)
            ch.did(pool.memset(fw[:, :], 0.0))
            pool.wait_ge(l_kc, 16)
            ch.sync()
            ch.did(pool.tensor_copy(fill[:, :, P:P + 1].bitcast(I32),
                                    kc[:, K_PAD:K_PAD + NS].bitcast(I32).rearrange("p (s a) -> p s a", a=1)))
            ch.did(pool.tensor_copy(XR[:, :, P:P + 1].bitcast(I32),
                                    kc[:, K_TOK:K_TOK + NT].bitcast(I32).rearrange("p (s a) -> p s a", a=1)))
            ch.sync()
            pool.dma_start(xslot.rearrange("(p s) r -> p (s r)", p=P),
                           fw[:, :]).then_inc(d_fill, 16)
            ch.did(pool.tensor_copy(alt[:, :, 0:1].bitcast(I32),
                                    kc[:, K_TOK2:K_TOK2 + NT].bitcast(I32).rearrange("p (s a) -> p s a", a=1)))
            pool.wait_ge(l_b, 16)
            ch.sync(pool.tensor_copy(bprt[:, 0, :], braw[:]))
            ch.sync(pool.tensor_tensor(bres[:], braw[:], bprt[:, 0, :], ALU.subtract))
            ch.sync(pool.tensor_copy(bprt[:, 1, :], bres[:]))
            ch.sync(pool.tensor_tensor(bres[:], bres[:], bprt[:, 1, :], ALU.subtract))
            pool.tensor_copy(bprt[:, 2, :], bres[:]).then_inc(k_bprt, 1)

            def norm(g):
                if norm_tiles(g, 1):
                    pool.wait_ge(s_rs, g // 2 + 1)
                    for t in norm_tiles(g, 1):
                        ins = pool.tensor_scalar(XR[:, t, 0:P], X[:, t, :], mv[:, t, 0:1], rstd[:, t:t + 1],
                                                 ALU.subtract, ALU.mult)
                    ins.then_inc(s_xp, 1)

            for g in range(NG):
                norm(g)
            ch.sync(pool.memset(keep[:, :, 0:1], 0.0))
            pool.sem_inc(k_keep, 1)
            pool.wait_ge(s_xt, 2 * NG)
            pool.wait_ge(k_wbd, 1)
            pool.tensor_tensor(Qv[:], xsum[:].rearrange("p (c a) -> p c a", a=1).to_broadcast([P, C, P]),
                               wbd[:, 2:3, :].to_broadcast([P, C, P]), ALU.mult).then_inc(s_q, 1)
            pool.wait_ge(d_fill, 16)
            for k in range(2):
                pool.wait_ge(s_idx, k + 1)
                pool.wait_ge(s_cw, 2 * k + 2)
                for h in range(2):
                    half = slice(h * NT // 2, (h + 1) * NT // 2)
                    if k == 1:
                        pool.wait_ge(d_sc[0][h], 16 * (NT // 2))
                        ch.sync(pool.tensor_copy(XR[:, half, P:ROW], alt[:, half, :]))
                    for t in range(half.start, half.stop):
                        pool.indirect_dma_start(xslot, bass.IndirectOffsetOnAxis(ap=idx[:, k, t:t + 1], axis=0),
                                                XR[:, t, :], None).then_inc(d_sc[k][h], 16)

            def run(j, u, fixed):
                if has(j + 1, fixed):
                    v = (u + 1) % UN
                    turn = (j + 1) // UN if fixed else None
                    pool.wait_ge(d_rx[v], 16 * (turn + 1) if fixed else j_turn(j, u, 1) * 16 + 16)
                    pool.wait_ge(d_y[v], 16 * turn if fixed else j_turn(j, u, 1) * 16)
                    gate()
                    pool.tensor_copy(meta[:, v, :], RX[:, v, P:ROW]).then_inc(r_meta, 1)
                if has(j - 3, fixed):
                    v = (u - 3) % UN
                    pool.wait_ge(r_y, j - 2)
                    pool.wait_ge(r_meta, j - 2)
                    gate()
                    pool.indirect_dma_start(ydram, bass.IndirectOffsetOnAxis(ap=meta[:, v, 0:1].bitcast(I32), axis=0),
                                            yb[:, v, :], None).then_inc(d_y[v], 16)

            steps(pool, run)
        @block.vector
        def _(dve):
            ch = Chain(dve, cd)
            def stats(q):
                dve.wait_ge(l_x[q], 16)
                for t in range(q * QT, (q + 1) * QT):
                    ins = dve.bn_stats(st[:, t, :], X[:, t, :])
                ch.sync(ins)
                for t in range(q * QT, (q + 1) * QT):
                    ins = dve.bn_aggr(mv[:, t, :], st[:, t, :])
                ins.then_inc(s_var, 1)

            def invert(q):
                dve.wait_ge(s_std, q + 1)
                v = rstd[:, q * QT:(q + 1) * QT]
                dve.reciprocal(v, v).then_inc(s_rs, 1)

            def norm(g):
                dve.wait_ge(s_rs, g // 2 + 1)
                for t in norm_tiles(g, 0):
                    ins = dve.tensor_scalar(XR[:, t, 0:P], X[:, t, :], mv[:, t, 0:1], rstd[:, t:t + 1],
                                            ALU.subtract, ALU.mult)
                ins.then_inc(s_xn, 1)

            def pick(half, logits, mx, r, m):
                ch.sync(dve.tensor_reduce(sm[:, mx, half], logits[:, half], AX.X, ALU.max))
                ch.sync(dve.tensor_tensor(eq[:, half], logits[:, half], over_e(sm[:, mx, half]), ALU.is_equal))
                ch.sync(dve.tensor_tensor(eq[:, half], eq[:, half], rev_b, ALU.mult))
                ch.sync(dve.tensor_reduce(sm[:, r, half], eq[:, half], AX.X, ALU.max))
                ch.sync(dve.tensor_tensor(m[:, half], over_e(sm[:, r, half]), rev_b, ALU.is_equal))

            def choose(h):
                half = slice(h * HT, (h + 1) * HT)
                dve.wait_ge(s_gl, (h + 1) * NG // 2)
                ch.sync(dve.tensor_tensor(lg[:, half], PS[:, G_BANK[h], 0:HT * NE].rearrange("p (t e) -> p t e", e=NE),
                                          gb[:].rearrange("p (a e) -> p a e", a=1).to_broadcast([P, HT, NE]), ALU.add))
                pick(half, lg, MX, R1, m1)
                dve.tensor_tensor(ex[:, half], lg[:, half], over_e(sm[:, MX, half]), ALU.subtract).then_inc(s_dl, 1)
                ch.sync(dve.scalar_tensor_tensor(out=lg2[:, half].rearrange("p t e -> p (t e)"),
                                                 in0=m1[:, half].rearrange("p t e -> p (t e)"), scalar=-BIG,
                                                 in1=lg[:, half].rearrange("p t e -> p (t e)"), op0=ALU.mult, op1=ALU.add))
                pick(half, lg2, MX2, R2, m2)
                ch.did(dve.tensor_tensor(mbf[:].rearrange("p e t -> p t e")[:, half], m1[:, half], m2[:, half], ALU.add))

            def weigh(h):
                half = slice(h * HT, (h + 1) * HT)
                dve.wait_ge(s_exg, h + 1)
                ch.did(dve.tensor_reduce(sm[:, SUM, half], ex[:, half], AX.X, ALU.add))
                ch.sync(dve.tensor_tensor(eq[:, half], ex[:, half], m2[:, half], ALU.mult))
                ch.did(dve.tensor_reduce(sm[:, CW2, half], eq[:, half], AX.X, ALU.add))
                ch.sync(dve.reciprocal(sm[:, CW1, half], sm[:, SUM, half]))
                dve.tensor_copy(XR[:, half, P + 1:P + 2], sm[:, CW1, half].rearrange("p (t a) -> p t a", a=1)).then_inc(s_cw, 1)
                dve.tensor_tensor(alt[:, half, 1:2], sm[:, CW2, half].rearrange("p (t a) -> p t a", a=1),
                                  sm[:, CW1, half].rearrange("p (t a) -> p t a", a=1), ALU.mult).then_inc(s_cw, 1)

            stats(0)
            invert(0)
            norm(0)
            stats(1)
            norm(1)
            invert(1)
            norm(2)
            stats(2)
            norm(3)
            invert(2)
            dve.wait_ge(l_ws, 48)
            dve.wait_ge(l_kc, 16)
            dve.tensor_tensor(wbd[:], wqk[:], kc[:, K_BLK:K_BLK + P].rearrange("p (a b) -> p a b", a=1)
                              .to_broadcast([P, 3, P]), ALU.mult).then_inc(k_wbd, 1)
            dve.tensor_copy(lbf[:], kc[:, K_U:K_U + P])
            dve.tensor_copy(obf[:], kc[:, K_ONE:K_ONE + P]).then_inc(k_bf, 1)
            norm(4)
            stats(3)
            norm(5)
            invert(3)
            norm(6)
            norm(7)
            choose(0)
            weigh(0)
            choose(1)
            ch.sync()
            dve.wait_ge(k_keep, 1)
            dve.tensor_tensor_scan(cum[:].rearrange("p e t -> p (e t)"), keep[:].rearrange("p e t -> p (e t)"),
                                   mbf[:].rearrange("p e t -> p (e t)"), 0.0, ALU.mult, ALU.add).then_inc(s_cum, 1)
            weigh(1)

            dve.wait_ge(s_tot, 1)
            ch.sync(dve.tensor_scalar(ntl[:], PS[:, 7, 0:NE], 127.0, None, ALU.add))
            ch.sync(dve.tensor_scalar(ntl[:], ntl[:], 7, None, ALU.arith_shift_right))
            ch.sync(dve.tensor_copy(se[:, TLF, :], ntl[:]))
            ch.sync(dve.tensor_tensor_scan(se[:, PIN, :], kc[:, K_ONE:K_ONE + NE], se[:, TLF, :], 0.0, ALU.mult, ALU.add))
            ch.sync(dve.tensor_tensor(se[:, BAS, :], se[:, PIN, :], se[:, TLF, :], ALU.subtract))
            ch.sync(dve.tensor_scalar(se[:, OFF, :], se[:, BAS, :], float(P), None, ALU.mult))
            dve.wait_ge(s_rk, 1)
            ch.sync(dve.tensor_tensor(slot[:], PS[:, 4, :].rearrange("p (e t) -> p t e", e=NE),
                                      se[:, OFF:OFF + 1, :].to_broadcast([P, NT, NE]), ALU.add))
            for k, (m, r) in enumerate(((m1, R1), (m2, R2))):
                ch.sync(dve.tensor_tensor(eq[:], slot[:], m[:], ALU.mult))
                ch.sync(dve.tensor_reduce(sm[:, r, :], eq[:], AX.X, ALU.add))
                dve.tensor_copy(idx[:, k, :], sm[:, r, :]).then_inc(s_idx, 1)

            def gated(g, b):
                for c, (_, m) in enumerate(SCH):
                    dve.wait_ge(s_sg, 2 * (g * NB + c) + 2)
                    dve.tensor_tensor(sS[0:m, b, c, :], sS[0:m, b, c, :], sG[0:m, b, c, :], ALU.mult).then_inc(s_sm, 1)

            def add_z(g, b):
                dve.wait_ge(s_z, g + 1)
                v = X[:, bass.ds(g * GT, GT), :].rearrange("p t e -> p (t e)")
                dve.tensor_tensor(v, PS[:, 4 + b, :], v, ALU.add).then_inc(s_za, 1)

            def attend(part):
                for k in range(CT):
                    c = part * CT + k
                    prv = pr[:, bass.ds(c, 1), :].rearrange("p a (b h) -> p (a b) h", b=2).rearrange(
                        "p b (h a) -> p b h a", a=1).to_broadcast([P, 2, H, D])
                    vbv = Vb[:, bass.ds(c, 1), :].rearrange("p a (h e) -> p a h e", h=H).to_broadcast([P, 2, H, D])
                    ins = dve.tensor_tensor(at[:, k].rearrange("p b (h e) -> p b h e", h=H), prv, vbv, ALU.mult)
                ins.then_inc(s_at, 1)
                dve.wait_ge(s_at, part + 1)
                xv = X[:, bass.ds(part * CT * 2, CT * 2), :].rearrange("p t e -> p (t e)")
                dve.tensor_tensor(xv, xv, at[:].rearrange("p k b e -> p (k b e)"), ALU.add).then_inc(s_ax, 1)

            def score(g):
                dve.wait_ge(s_y, g + 1)
                dve.tensor_tensor(prod[:, g % 2, :].rearrange("p (t e) -> p t e", t=GT),
                                  PS[:, 6 + g % 2, :].rearrange("p (t e) -> p t e", t=GT),
                                  XR[:, g * GT:(g + 1) * GT, 0:P], ALU.mult).then_inc(s_pr, 1)
                dve.wait_ge(s_pr, g + 1)
                ch.did(dve.tensor_reduce(sc[:, g * GT * H:(g + 1) * GT * H],
                                         prod[:, g % 2, :].rearrange("p (r d) -> p r d", d=D), AX.X, ALU.add))

            gated(0, 0)
            score(0)
            gated(1, 1)
            for g in range(1, NG):
                score(g)
            ch.sync(dve.tensor_tensor(
                ecmp[:], kc[0:1, K_TILE:K_TILE + NS].rearrange("p (s a) -> p s a", a=1).to_broadcast([1, NS, NE]),
                se[0:1, PIN:PIN + 1, :].to_broadcast([1, NS, NE]), ALU.is_ge))
            ch.sync(dve.tensor_reduce(emf[:], ecmp[:], AX.X, ALU.add))
            dve.tensor_scalar(emi[:], emf[:], float(NE - 1), None, ALU.min).then_inc(s_em, 1)
            ch.sync()
            sc_v = sc[:].rearrange("p (c r) -> p c r", c=C)
            mxa = se[:, 6:8, :].rearrange("p a e -> p (a e)")
            ch.sync(dve.tensor_reduce(mxa, sc_v.rearrange("p c r -> p r c"), AX.X, ALU.max))
            dve.tensor_tensor(sd[:], sc_v, mxa.rearrange("p (a r) -> p a r", a=1).to_broadcast([P, C, 2 * H]),
                              ALU.subtract).then_inc(s_ds, 1)
            dve.wait_ge(s_exa, 1)
            asum = se[:, 6:8, :].rearrange("p a e -> p (a e)")
            ch.sync(dve.tensor_reduce(asum, pr[:].rearrange("p c r -> p r c"), AX.X, ALU.add))
            ch.sync(dve.reciprocal(asum, asum))
            ch.sync(dve.tensor_tensor(pr[:], pr[:], asum.rearrange("p (a r) -> p a r", a=1).to_broadcast([P, C, 2 * H]), ALU.mult))
            dve.wait_ge(s_vb, C // GT)
            attend(0)
            dve.wait_ge(s_ax, 1)
            add_z(0, 0)
            add_z(1, 1)
            with dve.Fori(1, NG // 2) as it:
                for b in range(2):
                    gated(it * 2 + b, b)
                attend(it)
                dve.wait_ge(s_ax, it + 1)
                for b in range(2):
                    add_z(it * 2 + b, b)

            def run(j, u, fixed):
                if has(j - 0, fixed):
                    b = u % 2
                    dve.wait_ge(r_sg, j + 1)
                    dve.wait_ge(r_at, max(j - 1, 0) if fixed else j - 1)
                    dve.tensor_tensor(ra[:, b, :], sg[:, b, :], PS[:, 2 + b, F:F2], ALU.mult).then_inc(r_a, 1)
                if has(j - 2, fixed):
                    b, v = u % 2, (u - 2) % UN
                    dve.wait_ge(r_dn, j - 1)
                    dve.wait_ge(r_meta, j - 1)
                    if not fixed:
                        dve.wait_ge(d_y[v], j_turn(j, u, -2) * 16)
                    elif j - 2 >= UN:
                        dve.wait_ge(d_y[v], 16 * ((j - 2) // UN))
                    dve.tensor_scalar(yb[:, v, :], PS[:, 6 + b, 0:P], meta[:, v, 1:2], None, ALU.mult).then_inc(r_y, 1)

            steps(dve, run)
            def close(g, b, it, first):
                dve.wait_ge(d_yl[b], it * 16 + 16)
                if not first:
                    dve.wait_ge(d_o[b], it * 16)
                o = ob[:, b].rearrange("p (t e) -> p t e", t=GT)
                dve.tensor_tensor(o, yl[:, b, :, 0, :], X[:, bass.ds(g * GT, GT), :], ALU.add).then_inc(s_f1, 1)
                dve.wait_ge(s_f1, g + 1)
                dve.tensor_tensor(o, o, yl[:, b, :, 1, :], ALU.add).then_inc(s_f2, 1)

            for b in range(YL):
                close(b, b, 0, True)
            with dve.Fori(1, NG // YL) as it:
                for b in range(YL):
                    close(it * YL + b, b, it, False)

        @block.scalar
        def _(act):
            act.dma_start(braw[:], d["biases"]).then_inc(l_b, 16)
            act.dma_start(kc[:], d["kc"]).then_inc(l_kc, 16)
            act.dma_start(wqk[:].rearrange("p a b -> p (a b)"), d["wqk"]).then_inc(l_ws, 16)
            act.dma_start(gw[:], d["gate_w"]).then_inc(l_ws, 16)
            act.dma_start(gb[:], d["gate_b"].to_broadcast([P, NE])).then_inc(l_ws, 16)
            act.dma_start(sw1[:], d["sw1"]).then_inc(l_sh, 16)
            act.dma_start(sw3[:], d["sw3"]).then_inc(l_sh, 16)
            act.dma_start(sw2[:, 0:2, :], d["sw2"][0:256, :].rearrange("(c p) n -> p c n", p=P)).then_inc(l_sh, 16)
            act.dma_start(sw2[0:96, 2, :], d["sw2"][256:SF, :]).then_inc(l_sh, 16)
            act.dma_start(sbc[:, 0:2, :], d["sb_a"]).then_inc(l_sh, 16)
            act.dma_start(sbc[0:96, 2:3, :], d["sb_b"]).then_inc(l_sh, 16)
            def deviation(q):
                act.wait_ge(s_var, q + 1)
                act.activation(rstd[:, q * QT:(q + 1) * QT], mv[:, q * QT:(q + 1) * QT, 1], ACT.Sqrt,
                               bias=kc[:, K_EPS:K_EPS + 1]).then_inc(s_std, 1)

            act.wait_ge(l_kc, 16)
            deviation(0)
            for g in range(NG):
                if g % 2 == 0 and g // 2 + 1 < NQ:
                    deviation(g // 2 + 1)
                act.wait_ge(s_tp, g + 1)
                for k in range(2):
                    act.activation(xnT[:, g * GW + k * T:g * GW + (k + 1) * T], PS[:, g % 2, k * T:(k + 1) * T],
                                   ACT.Copy, accum_out=xsum[:, 2 * g + k:2 * g + k + 1]).then_inc(s_xt, 1)
                if g == NG // 2:
                    act.wait_ge(k_mbd, 1)
                    act.activation(mbd[:], PS[:, 6, 0:P], ACT.Copy).then_inc(k_mbd, 1)
            act.wait_ge(l_sh, 96)

            def gates(g, b, c):
                m = SCH[c][1]
                k = (c + b) % 2
                act.wait_ge(s_up, g * NB + c + 1)
                act.activation(sS[0:m, b, c, :], PS[0:m, k, :], ACT.Silu, bias=sbc[0:m, c, 0:1]).then_inc(s_sg, 1)
                act.activation(sG[0:m, b, c, :], PS[0:m, 2 + k, :], ACT.Identity, bias=sbc[0:m, c, 1:2]).then_inc(s_sg, 1)

            for h in range(2):
                act.wait_ge(s_dl, h + 1)
                v = ex[:, h * HT:(h + 1) * HT, :].rearrange("p t e -> p (t e)")
                act.activation(v, v, ACT.Exp).then_inc(s_exg, 1)
            for n in range(2 * NB):
                gates(n // NB, n // NB, n % NB)
            act.wait_ge(k_bprt, 1)
            for k in range(3):
                act.dma_start(bdram[k].rearrange("(p w) -> p w", p=P), bprt[:, k, :]).then_inc(d_bst, 16)
            act.wait_ge(d_bst, 48)
            act.dma_start(bsp[:], bdram).then_inc(d_bld, 16)
            for q in range(C // GT):
                act.wait_ge(s_v, q + 1)
                act.activation(Vb[:, GT * q:GT * q + GT, :].rearrange("p c e -> p (c e)"), PS[:, 6, :],
                               ACT.Copy).then_inc(s_vb, 1)
            act.wait_ge(s_ds, 1)
            act.activation(pr[:].rearrange("p c r -> p (c r)"), sd[:].rearrange("p c r -> p (c r)"), ACT.Exp,
                           scale=float(P) ** -0.5).then_inc(s_exa, 1)
            with act.Fori(1, NG // 2) as it:
                for b in range(2):
                    act.wait_ge(s_z, it * 2 + b - 1)
                    for c in range(NB):
                        gates(it * 2 + b, b, c)

            def run(j, u, fixed):
                if has(j + 1, fixed):
                    b = (u + 1) % 2
                    act.wait_ge(r_tp, j + 2)
                    act.wait_ge(r_up, max(j, 0) if fixed else j)
                    act.activation(rxT[:, b, :], PS[:, b, 0:P], ACT.Copy).then_inc(r_xt, 1)
                if has(j, fixed):
                    b = u % 2
                    act.wait_ge(r_up, j + 1)
                    act.wait_ge(r_a, max(j - 1, 0) if fixed else j - 1)
                    act.activation(sg[:, b, :], PS[:, 2 + b, 0:F], ACT.Silu).then_inc(r_sg, 1)
                if has(j - 1, fixed):
                    b = (u - 1) % 2
                    act.wait_ge(r_at, j)
                    act.wait_ge(r_dn, max(j - 2, 0) if fixed else j - 2)
                    act.activation(raT[:, b, :], PS[0:FH, 4 + b, 0:2 * P], ACT.Copy).then_inc(r_att, 1)

            steps(act, run)
            with act.Fori(0, NG // YL) as it:
                for b in range(YL):
                    g = it * YL + b
                    act.wait_ge(s_f2, g + 1)
                    act.dma_start(out_v[:, bass.ds(g * GT, GT), :], ob[:, b, :].rearrange("p (t e) -> p t e", t=GT)).then_inc(d_o[b], 16)

        @block.tensor
        def _(pe):
            pe.wait_ge(l_kc, 16)

            def turn(g):
                pe.wait_ge(s_xn, g + 1)
                if norm_tiles(g, 1):
                    pe.wait_ge(s_xp, g - 1)
                if g >= 2:
                    pe.wait_ge(s_xt, 2 * g - 2)
                for t in range(GT):
                    ins = pe.transpose(PS[:, g % 2, t * P:(t + 1) * P], XR[:, g * GT + t, 0:P], ident)
                ins.then_inc(s_tp, 1)

            def logits(g):
                pe.wait_ge(s_xt, 2 * g + 2)
                for t in range(g * GT, (g + 1) * GT):
                    k = t % HT
                    ins = pe.matmul(PS[:, G_BANK[t // HT], k * NE:(k + 1) * NE], xnT[:, t * P:(t + 1) * P], gw[:], start=True, stop=True)
                ins.then_inc(s_gl, 1)

            def project(g):
                if g >= 2:
                    pe.wait_ge(s_pr, g - 1)
                for t in range(GT):
                    tile = g * GT + t
                    ins = pe.matmul(PS[:, 6 + g % 2, t * P:(t + 1) * P], xnT[:, tile * P:(tile + 1) * P], mbd[:],
                                    start=True, stop=True)
                ins.then_inc(s_y, 1)

            def values(q):
                pe.wait_ge(s_q, 1)
                pe.wait_ge(s_pr, NG)
                pe.wait_ge(s_vb, q)
                pe.matmul(PS[:, 6, :], kc[:, K_ONE:K_ONE + P], Qv[:, GT * q:GT * q + GT, :].rearrange("p c e -> p (c e)"),
                          start=True, stop=True).then_inc(s_v, 1)

            def up(g, b, c, first):
                f, m = SCH[c]
                k = (c + b) % 2
                if not first:
                    pe.wait_ge(s_sg, 2 * (g * NB + c) - 2)
                xv = xnT[:, bass.ds(g * GW, GW)]
                pe.matmul(PS[0:m, k, :], sw1[:, f:f + m], xv, start=True, stop=True)
                pe.matmul(PS[0:m, 2 + k, :], sw3[:, f:f + m], xv, start=True, stop=True).then_inc(s_up, 1)

            def down(g, b, first):
                pe.wait_ge(s_sm, g * NB + NB)
                if not first:
                    pe.wait_ge(s_za, g - 1)
                for t in range(GT):
                    zt = PS[:, 4 + b, t * P:(t + 1) * P]
                    pe.matmul(zt, obf[0:3, :], bsp[:, NBIAS - P:NBIAS], start=True, stop=False)
                    for c, (_, m) in enumerate(SCH):
                        ins = pe.matmul(zt, sS[0:m, b, c, t * P:(t + 1) * P], sw2[0:m, c, :], start=False, stop=(c == NB - 1))
                ins.then_inc(s_z, 1)

            turn(0)
            turn(1)
            pe.wait_ge(l_ws, 48)
            for g in range(NG):
                logits(g)
                if g == NG // 2 - 1:
                    pe.wait_ge(k_wbd, 1)
                    pe.matmul(PS[:, 6, 0:P], wbd[:, 0, :], wbd[:, 1, :], start=True, stop=True).then_inc(k_mbd, 1)
                if g + 2 < NG:
                    turn(g + 2)
            pe.wait_ge(l_sh, 96)
            for n in range(2 * NB):
                if n == 4:
                    pe.wait_ge(k_bf, 1)
                    pe.wait_ge(s_cum, 1)
                    pe.matmul(PS[:, 7, 0:NE], obf[:], cum[:, :, NT - 1], start=True, stop=True).then_inc(s_tot, 1)
                    pe.matmul(PS[:, 4, :], lbf[:], mbf[:].rearrange("p e t -> p (e t)"), start=True, stop=False)
                    pe.matmul(PS[:, 4, :], obf[:], cum[:].rearrange("p e t -> p (e t)"), start=False, stop=True).then_inc(s_rk, 1)
                up(n // NB, n // NB, n % NB, n < 2)
            pe.wait_ge(k_mbd, 2)
            pe.wait_ge(s_idx, 1)
            project(0)
            project(1)
            pe.wait_ge(d_bld, 16)
            down(0, 0, True)
            project(2)
            project(3)
            down(1, 1, True)
            for g in range(4, NG):
                project(g)
            for q in range(C // GT):
                values(q)
            with pe.Fori(1, NG // 2) as it:
                for b in range(2):
                    for c in range(NB):
                        up(it * 2 + b, b, c, False)
                for b in range(2):
                    down(it * 2 + b, b, False)

            pe.wait_ge(l_w13, 16)
            pe.wait_ge(l_w2, 16)
            pe.wait_ge(s_em, 1)
            pe.wait_ge(s_sg, 2 * NG * NB)
            pe.wait_ge(s_za, NG)

            held = [pe.alloc_register(f"expert{v}") for v in range(UN)]

            def read_expert(j, u):
                at = slice(j, j + 1) if isinstance(j, int) else bass.ds(j, 1)
                pe.reg_load(held[u % UN], emi[0:1, at])

            def expert(u):
                return pe.snap(held[u % UN], min_val=0, max_val=NE - 1)

            def run(j, u, fixed):
                if has(j + 1, fixed):
                    b, v = (u + 1) % 2, (u + 1) % UN
                    pe.wait_ge(d_rx[v], 16 * ((j + 1) // UN + 1) if fixed else j_turn(j, u, 1) * 16 + 16)
                    pe.transpose(PS[:, b, 0:P], RX[:, v, 0:P], ident).then_inc(r_tp, 1)
                if has(j, fixed):
                    b = u % 2
                    e = expert(u)
                    pe.wait_ge(r_xt, j + 1)
                    pe.matmul(PS[:, 2 + b, 0:F2], obf[0:3, :], bsp[:, bass.ds(e * F2, F2)], start=True, stop=False)
                    pe.matmul(PS[:, 2 + b, 0:F2], rxT[:, b, :], w13[:, bass.ds(e * F2, F2)], start=False,
                              stop=True).then_inc(r_up, 1)
                    if has(j + 1, fixed):
                        read_expert(j + 1, u + 1)
                if has(j - 1, fixed):
                    b = (u - 1) % 2
                    pe.wait_ge(r_a, j)
                    pe.transpose(PS[0:FH, 4 + b, 0:P], ra[:, b, 0:FH], ident)
                    pe.transpose(PS[0:FH, 4 + b, P:2 * P], ra[:, b, FH:F], ident).then_inc(r_at, 1)
                if has(j - 2, fixed):
                    b = u % 2
                    e = expert(u - 2)
                    pe.wait_ge(r_att, j - 1)
                    pe.wait_ge(r_y, max(j - 3, 0) if fixed else j - 3)
                    pe.matmul(PS[:, 6 + b, 0:P], obf[0:3, :], bsp[:, bass.ds(e * P + NE * F2, P)], start=True, stop=False)
                    for k in range(2):
                        ins = pe.matmul(PS[:, 6 + b, 0:P], raT[:, b, k * P:(k + 1) * P],
                                        w2[:, bass.ds(e * 2 * P + k * P, P)], start=False, stop=(k == 1))
                    ins.then_inc(r_dn, 1)

            read_expert(0, 0)
            steps(pe, run)


def constants():
    import numpy as np
    k = np.zeros((P, KW), np.float32)
    i, j = np.arange(P)[:, None], np.arange(P)[None, :]
    k[:, K_ID:K_ID + P] = i == j
    k[:, K_BLK:K_BLK + P] = i // D == j // D
    k[:, K_U:K_U + P] = -1.0 * (i >= j)
    k[:, K_ONE:K_ONE + P] = 1
    k[:, K_REV:K_REV + NE] = NE - np.arange(NE)
    k[:, K_TILE:K_TILE + NS] = np.arange(NS)
    kb = k.view(np.int32)
    kb[:, K_TOK:K_TOK + NT] = (i * NT + np.arange(NT)[None, :]) * 2
    kb[:, K_TOK2:K_TOK2 + NT] = kb[:, K_TOK:K_TOK + NT] + 1
    kb[:, K_PAD:K_PAD + NS] = 2 * N + i * NS + np.arange(NS)[None, :]
    k[:, K_EPS] = EPS
    return k


def arrays_of(inp):
    import numpy as np
    a = {n: np.asarray(v) for n, v in inp.items()}
    f = "L0_ffn_"
    w13 = np.concatenate([a[f + "w1"], a[f + "w3"]], axis=2)
    b13 = np.concatenate([a[f + "b1"], a[f + "b3"]], axis=1)
    r = {
        "x": a["L0_attn_x"].reshape(N, P),
        "kc": constants(),
        "wqk": np.concatenate([np.tile(a["L0_attn_Wq"], (H, H)), np.tile(a["L0_attn_Wk"], (H, H)),
                               np.tile(a["L0_attn_Wv"].T, (H, H))], axis=1),
        "gate_w": a[f + "gate_w"], "gate_b": a[f + "gate_b"].reshape(1, NE),
        "biases": np.concatenate([b13.reshape(-1), a[f + "b2"].reshape(-1), a[f + "sb2"]]).reshape(P, NBIAS // P),
        "sw1": a[f + "sw1"], "sw3": a[f + "sw3"], "sw2": a[f + "sw2"],
        "sb_a": np.stack([a[f + "sb1"][:256].reshape(2, P).T, a[f + "sb3"][:256].reshape(2, P).T], axis=2),
        "sb_b": np.stack([a[f + "sb1"][256:], a[f + "sb3"][256:]], axis=1)[:, None, :],
        "w13": w13.transpose(1, 0, 2).reshape(P, NE * F2),
        "w2": a[f + "w2"].reshape(NE, 2, FH, P).transpose(2, 0, 1, 3).reshape(FH, NE * 2 * P),
    }
    return {n: np.ascontiguousarray(v) for n, v in r.items()}


def program(nc, arrays):
    d = {n: nc.dram_tensor(f"in_{n}", v.shape, mybir.dt.from_np(v.dtype), kind="ExternalInput").ap()
         for n, v in arrays.items()}
    d["out"] = nc.dram_tensor("out_0", (N, P), F32, kind="ExternalOutput").ap()
    build(nc, d)


def kernel(**inputs):
    import concourse.bacc as bacc
    from concourse.bass_utils import run_bass_kernel_spmd
    arrays = arrays_of(inputs)
    nc = bacc.Bacc("TRN2", target_bir_lowering=False, num_devices=1)
    program(nc, arrays)
    r = run_bass_kernel_spmd(nc, [{f"in_{n}": v for n, v in arrays.items()}], core_ids=[0])
    return r.results[0]["out_0"].reshape(C, T, P)
```

```python
import concourse.bass as bass
from concourse import mybir
from contextlib import ExitStack

ALU = mybir.AluOpType
ACT = mybir.ActivationFunctionType
AX = mybir.AxisListType
F32 = mybir.dt.float32
F32R = mybir.dt.float32r
BF16 = mybir.dt.bfloat16
I32 = mybir.dt.int32

P = 128
C, T = 16, 256
N = C * T
NT = N // P
GT = 4
NG = NT // GT
GW = GT * P
NQ = NG // 2
QT = 2 * GT
NPOOL = 1
HT = NT // 2
H, D = 16, 8
NE, F = 16, 176
FH = F // 2
F2 = 2 * F
SF = 352
SCH = [(0, 128), (128, 128), (256, 96)]
NB = len(SCH)
CT = C // (NG // 2)
NS = (2 * N + NE * (P - 1)) // P
UN = 8
ROW = P + 2
CL, NC = 2, NT // 2
YL = 8
EARLY = ((2, 3), (5, 6))
EG = 7
ER = 2
G_BANK = (4, 7)
EPS = 1e-5
BIG = 3.0e38
WQ = NE * F2 // NQ
NBIAS = NE * (F2 + P) + P

K_ID, K_BLK, K_U, K_ONE = 0, 128, 256, 384
K_REV = 512
K_TILE = K_REV + NE
K_TOK = K_TILE + NS
K_TOK2 = K_TOK + NT
K_PAD = K_TOK2 + NT
KW = K_PAD + NS
NY = 2 * N + NS * P


class Chain:

    def __init__(self, eng, sem):
        self.eng, self.sem, self.base, self.n = eng, sem, 0, 0

    def did(self, ins):
        ins.then_inc(self.sem, 1)
        self.n += 1

    def sync(self, ins=None):
        if ins is not None:
            self.did(ins)
        self.eng.wait_ge(self.sem, self.base + self.n)

    def turn(self, start, it, per):
        self.base, self.n = start + it * per, 0

    def after(self, total):
        self.base, self.n = 0, total


def build(nc, d):
    ctx = ExitStack()
    with ctx:
        def sb(name, shape, dt=F32):
            return ctx.enter_context(nc.sbuf_tensor(name, shape, dt))

        def sem(name):
            return ctx.enter_context(nc.semaphore(name))

        xslot = nc.dram_tensor("xslot", (NS * P, ROW), F32).ap()
        ydram = nc.dram_tensor("ydram", (NY, P), F32).ap()
        vdram = nc.dram_tensor("vdram", (1, C * P), F32).ap()
        bdram = nc.dram_tensor("bdram", (3, NBIAS), BF16).ap()

        kc = sb("kc", [P, KW])
        lbf = sb("lbf", [P, P], BF16)
        obf = sb("obf", [P, P], BF16)
        X = sb("X", [P, NT, P])
        XR = sb("XR", [P, NT, ROW])
        xnT = sb("xnT", [P, N])
        prod = sb("prod", [P, 2, GW])
        st = sb("st", [P, NT, 6])
        mv = sb("mv", [P, NT, 2])
        rstd = sb("rstd", [P, NT])
        eps = sb("eps", [P, 2])
        xsum = sb("xsum", [P, C])
        wqk = sb("wqk", [P, 3, P])
        wbd = sb("wbd", [P, 3, P])
        mbd = sb("mbd", [P, P])
        gw = sb("gw", [P, NE])
        gb = sb("gb", [P, NE])
        sw1 = sb("sw1", [P, SF])
        sw3 = sb("sw3", [P, SF])
        sw2 = sb("sw2", [P, NB, P])
        sbc = sb("sbc", [P, NB, 2])
        fw = sb("fw", [P, NS * ROW])
        fill = fw[:, :].rearrange("p (s r) -> p s r", r=ROW)
        w13 = fw[:, 0:NE * F2]
        w2 = fw[0:FH, NE * F2:NE * (F2 + 2 * P)]
        braw = sb("braw", [P, NBIAS // P])
        bres = sb("bres", [P, NBIAS // P])
        bprt = sb("bprt", [P, 3, NBIAS // P], BF16)
        w13h = sb("w13h", [P, NE * F2], F32R)
        w13l = sb("w13l", [P, NE * F2], F32R)
        rxh = sb("rxh", [P, 2, P], F32R)
        rxl = sb("rxl", [P, 2, P], F32R)
        bsh = sb("bsh", [3, P], BF16)
        bsp = XR[0:3].rearrange("p t r -> p (t r)")[:, 0:(NBIAS - P) // 2].bitcast(BF16)
        sc = sb("sc", [P, NT * H])
        sd = sb("sd", [P, C, 2 * H])
        pr = sb("pr", [P, C, 2 * H])
        at = sb("at", [P, CT, 2, P])
        alt = sb("alt", [P, NT, 2])
        mbf = sb("mbf", [P, NE, NT], BF16)
        cum = sb("cum", [P, NE, NT], BF16)
        gate = sb("gate", [P, 8, NT * NE])
        lg, ex, lg2, m1, m2, eq, slot = (gate[:, k].rearrange("p (t e) -> p t e", e=NE) for k in range(7))
        keep = gate[:, 7].rearrange("p (e t) -> p e t", t=NT)
        Vb = gate[:, 0:4].rearrange("p k w -> p (k w)").rearrange("p (c e) -> p c e", c=C)
        sm = sb("sm", [P, 8, NT])
        se = sb("se", [P, 8, NE])
        ntl = sb("ntl", [P, NE], I32)
        idx = sb("idx", [P, 2, NT], I32)
        emf = sb("emf", [1, NS])
        emi = sb("emi", [1, NS], I32)
        sS = sb("sS", [P, 2, NB, GW])
        sG = sb("sG", [P, 2, NB, GW])
        ecmp = prod[0:1].rearrange("p b w -> p (b w)").bitcast(BF16)[:, 0:NS * NE].rearrange("p (s e) -> p s e", e=NE)
        vS = sb("vS", [C, P])
        yl = XR[:].rearrange("p t r -> p (t r)")[:, 0:YL * 2 * CL * P].rearrange("p (b t k e) -> p b t k e", b=YL, k=2, e=P)
        ob = sS[:].rearrange("p b c w -> p (b c w)")[:, 0:YL * CL * P].rearrange("p (b w) -> p b w", b=YL)
        RX = fw[:, 0:UN * ROW].rearrange("p (u r) -> p u r", r=ROW)
        meta = sb("meta", [P, UN, 2])
        prod_w = prod[:].rearrange("p b w -> p (b w)")
        sg = prod_w[:, 2 * P:2 * P + 2 * F].rearrange("p (b w) -> p b w", b=2)
        ra = prod_w[:, 2 * P + 2 * F:2 * P + 4 * F].rearrange("p (b w) -> p b w", b=2)
        Wk = fw[:, UN * ROW:UN * ROW + (UN + 4) * P]
        yb = Wk[:, 0:UN * P].rearrange("p (u e) -> p u e", e=P)
        raT = Wk[0:FH, UN * P:(UN + 4) * P].rearrange("p (b w) -> p b w", b=2)

        PS = ctx.enter_context(nc.psum_tensor("PS", [P, 8, 512], F32))
        MX, MX2, R1, R2, SUM, CW1, CW2 = range(7)
        NEX, TLF, PIN, BAS, OFF = range(5)

        ident = kc[:, K_ID:K_ID + P]
        rev_b = kc[:, K_REV:K_REV + NE].rearrange("p (a e) -> p a e", a=1).to_broadcast([P, HT, NE])

        def over_e(col):
            return col.rearrange("p (t a) -> p t a", a=1).to_broadcast([P, HT, NE])

        def norm_tiles(g, mine):
            cut = (g + 1) * GT - (NPOOL if g >= 2 else 0)
            return range(cut, (g + 1) * GT) if mine else range(g * GT, cut)

        l_x = [sem(f"l_x{g}") for g in range(NG // 2)]
        l_kc, l_gate, l_ws, l_sh, l_w13, l_w2, l_b = (sem(n) for n in ("l_kc", "l_gate", "l_ws", "l_sh", "l_w13", "l_w2", "l_b"))
        cd, cp = sem("cd"), sem("cp")
        k_bf, k_wbd, k_mbd, k_bprt, k_keep, k_eps = (sem(n) for n in ("k_bf", "k_wbd", "k_mbd", "k_bprt", "k_keep", "k_eps"))
        d_bst, d_bld, d_fill, d_vs, d_vb = (sem(n) for n in ("d_bst", "d_bld", "d_fill", "d_vs", "d_vb"))
        s_var, s_std, s_rs, s_xn, s_xp, s_tp, s_xt = (sem(n) for n in ("s_var", "s_std", "s_rs", "s_xn", "s_xp", "s_tp", "s_xt"))
        s_gl, s_y, s_pr = (sem(n) for n in ("s_gl", "s_y", "s_pr"))
        s_dl, s_ds, s_exg, s_exa, s_v, s_vs = (sem(n) for n in ("s_dl", "s_ds", "s_exg", "s_exa", "s_v", "s_vs"))
        s_cum, s_tot, s_rk, s_em, s_idx, s_cw = (sem(n) for n in ("s_cum", "s_tot", "s_rk", "s_em", "s_idx", "s_cw"))
        s_up, s_sg, s_si, s_sm, s_z, s_za = (sem(n) for n in ("s_up", "s_sg", "s_si", "s_sm", "s_z", "s_za"))
        s_at, s_ax = sem("s_at"), sem("s_ax")
        d_sc = [[sem(f"d_sc{k}{h}") for h in range(2)] for k in range(2)]
        d_rx = [sem(f"d_rx{u}") for u in range(UN)]
        d_y = [sem(f"d_y{u}") for u in range(UN)]
        r_meta, r_tp, r_xh, r_xl, r_up, r_sg, r_a, r_at, r_att, r_dn, r_y = (
            sem(n) for n in ("r_meta", "r_tp", "r_xh", "r_xl", "r_up", "r_sg", "r_a", "r_at", "r_att", "r_dn", "r_y"))
        d_yl = [sem(f"d_yl{b}") for b in range(YL)]
        d_o = [sem(f"d_o{b}") for b in range(YL)]
        p_gate = sem("p_gate")
        s_wh, s_wl = sem("s_wh"), sem("s_wl")
        s_f1, s_f2 = sem("s_f1"), sem("s_f2")

        x_v = d["x"].rearrange("(t p) e -> p t e", p=P)
        out_v = d["out"].rearrange("(t p) e -> p t e", p=P)
        y_v = ydram[0:2 * N, :].rearrange("(p t k) e -> p t k e", t=NT, k=2)
        xs_v = xslot.rearrange("(s p) r -> s p r", p=P)

        def j_turn(j, u, ahead):
            return loop_it[0] + (u + ahead) // UN

        loop_it = [None]

        def steps(eng, run):
            turns = (NS - 4) // UN
            for j in range(-1, 3 + UN):
                run(j, j, True)
            with eng.Fori(1, turns) as it:
                loop_it[0] = it
                for u in range(3, 3 + UN):
                    run(it * UN + u, u, False)
            for j in range(3 + turns * UN, NS + 4):
                run(j, j, True)

        def has(j, fixed):
            return not fixed or 0 <= j < NS

        block = ctx.enter_context(nc.Block())

        @block.sync
        def _(sp):
            def load_x(g):
                two = slice(g * QT, (g + 1) * QT)
                sp.dma_start(X[:, two, :], x_v[:, two, :]).then_inc(l_x[g], 16)

            load_x(0)
            sp.dma_start(kc[:], d["kc"]).then_inc(l_kc, 16)
            sp.dma_start(gw[:], d["gate_w"]).then_inc(l_gate, 16)
            sp.dma_start(gb[:], d["gate_b"].to_broadcast([P, NE])).then_inc(l_gate, 16)
            load_x(1)
            sp.dma_start(wqk[:].rearrange("p a b -> p (a b)"), d["wqk"]).then_inc(l_ws, 16)
            load_x(2)
            load_x(3)
            sp.dma_start(sw1[:], d["sw1"]).then_inc(l_sh, 16)
            sp.dma_start(sw3[:], d["sw3"]).then_inc(l_sh, 16)
            sp.dma_start(sw2[:, 0:2, :], d["sw2"][0:256, :].rearrange("(c p) n -> p c n", p=P)).then_inc(l_sh, 16)
            sp.dma_start(sw2[0:96, 2, :], d["sw2"][256:SF, :]).then_inc(l_sh, 16)
            sp.dma_start(sbc[:, 0:2, :], d["sb_a"]).then_inc(l_sh, 16)
            sp.dma_start(sbc[0:96, 2:3, :], d["sb_b"]).then_inc(l_sh, 16)
            sp.dma_start(braw[:], d["biases"]).then_inc(l_b, 16)
            sp.wait_ge(k_bprt, 1)
            for k in range(3):
                sp.dma_start(bdram[k].rearrange("(p w) -> p w", p=P), bprt[:, k, :]).then_inc(d_bst, 16)
            sp.wait_ge(d_bst, 48)
            sp.dma_start(bsh[:], bdram[:, NBIAS - P:NBIAS]).then_inc(d_bld, 16)
            sp.wait_ge(d_fill, 16)
            sp.dma_start(w13, d["w13"]).then_inc(l_w13, 16)
            sp.dma_start(w2, d["w2"]).then_inc(l_w2, 16)
            sp.wait_ge(s_vs, 1)
            sp.dma_start(vdram.rearrange("a (c e) -> (a c) e", c=C), vS[:]).then_inc(d_vs, 16)
            sp.wait_ge(d_vs, 16)
            sp.wait_ge(s_idx, 4)
            sp.dma_start(Vb.rearrange("p c e -> p (c e)"), vdram.to_broadcast([P, C * P])).then_inc(d_vb, 16)
            for k in range(2):
                for h in range(2):
                    sp.wait_ge(d_sc[k][h], 16 * (NT // 2))

            def load(j, u, turn):
                if turn is not None:
                    sp.wait_ge(r_tp, j - UN + 1)
                    sp.wait_ge(r_meta, j - UN + 1)
                sp.dma_start(RX[:, u, :], xs_v[j]).then_inc(d_rx[u], 16)

            sp.wait_ge(s_wl, NQ)
            for u in range(UN):
                load(u, u, None)
                if u == 0:
                    sp.wait_ge(s_pr, NG)
                    sp.dma_start(bsp, bdram[:, 0:NBIAS - P]).then_inc(d_bld, 16)
            with sp.Fori(0, NS // UN - 1) as it:
                for u in range(UN):
                    load((it + 1) * UN + u, u, it)
            for j in range(NS - NS % UN, NS):
                load(j, j % UN, j // UN)
            for u in range(UN):
                sp.wait_ge(d_y[u], 16 * ((NS - u + UN - 1) // UN))

            def fetch(g, b):
                sp.dma_start(yl[:, b], y_v[:, bass.ds(g * CL, CL), :, :]).then_inc(d_yl[b], 16)

            for b in range(YL):
                fetch(b, b)
            with sp.Fori(0, NC // YL - 1) as it:
                for b in range(YL):
                    sp.wait_ge(s_f2, it * YL + b + 1)
                    fetch(it * YL + YL + b, b)
            for b in range(YL):
                sp.wait_ge(d_o[b], 16 * (NC // YL))

        @block.gpsimd
        def _(pool):
            ch = Chain(pool, cp)

            def gate():
                pool.sem_inc(p_gate, 1)

            pool.memset(keep, 1.0)
            ch.did(pool.memset(fw[:, :], 0.0))
            pool.wait_ge(l_kc, 16)
            ch.sync()
            ch.did(pool.tensor_copy(fill[:, :, P:P + 1].bitcast(I32),
                                    kc[:, K_PAD:K_PAD + NS].bitcast(I32).rearrange("p (s a) -> p s a", a=1)))
            ch.did(pool.tensor_copy(XR[:, :, P:P + 1].bitcast(I32),
                                    kc[:, K_TOK:K_TOK + NT].bitcast(I32).rearrange("p (s a) -> p s a", a=1)))
            ch.sync()
            pool.dma_start(xslot.rearrange("(p s) r -> p (s r)", p=P),
                           fw[:, :]).then_inc(d_fill, 16)
            ch.did(pool.tensor_copy(alt[:, :, 0:1].bitcast(I32),
                                    kc[:, K_TOK2:K_TOK2 + NT].bitcast(I32).rearrange("p (s a) -> p s a", a=1)))
            pool.wait_ge(l_b, 16)
            ch.sync(pool.tensor_copy(bprt[:, 0, :], braw[:]))
            ch.sync(pool.tensor_tensor(bres[:], braw[:], bprt[:, 0, :], ALU.subtract))
            ch.sync(pool.tensor_copy(bprt[:, 1, :], bres[:]))
            ch.sync(pool.tensor_tensor(bres[:], bres[:], bprt[:, 1, :], ALU.subtract))
            pool.tensor_copy(bprt[:, 2, :], bres[:]).then_inc(k_bprt, 1)

            def norm(g):
                if norm_tiles(g, 1):
                    pool.wait_ge(s_rs, g // 2 + 1)
                    for t in norm_tiles(g, 1):
                        ins = pool.tensor_scalar(XR[:, t, 0:P], X[:, t, :], mv[:, t, 0:1], rstd[:, t:t + 1],
                                                 ALU.subtract, ALU.mult)
                    ins.then_inc(s_xp, 1)

            for g in range(NG):
                norm(g)
            ch.sync(pool.memset(keep[:, :, 0:1], 0.0))
            pool.sem_inc(k_keep, 1)
            pool.wait_ge(d_fill, 16)
            for k in range(2):
                for h in range(2):
                    half = slice(h * NT // 2, (h + 1) * NT // 2)
                    pool.wait_ge(s_idx, 2 * k + h + 1)
                    pool.wait_ge(s_cw, 2 * h + k + 1)
                    if k == 1:
                        pool.wait_ge(d_sc[0][h], 16 * (NT // 2))
                        ch.sync(pool.tensor_copy(XR[:, half, P:ROW], alt[:, half, :]))
                    for t in range(half.start, half.stop):
                        pool.indirect_dma_start(xslot, bass.IndirectOffsetOnAxis(ap=idx[:, k, t:t + 1], axis=0),
                                                XR[:, t, :], None).then_inc(d_sc[k][h], 16)

            def run(j, u, fixed):
                if has(j + 1, fixed):
                    v = (u + 1) % UN
                    turn = (j + 1) // UN if fixed else None
                    pool.wait_ge(d_rx[v], 16 * (turn + 1) if fixed else j_turn(j, u, 1) * 16 + 16)
                    pool.wait_ge(d_y[v], 16 * turn if fixed else j_turn(j, u, 1) * 16)
                    gate()
                    pool.tensor_copy(meta[:, v, :], RX[:, v, P:ROW]).then_inc(r_meta, 1)
                if has(j - 3, fixed):
                    v = (u - 3) % UN
                    pool.wait_ge(r_y, j - 2)
                    pool.wait_ge(r_meta, j - 2)
                    gate()
                    pool.indirect_dma_start(ydram, bass.IndirectOffsetOnAxis(ap=meta[:, v, 0:1].bitcast(I32), axis=0),
                                            yb[:, v, :], None).then_inc(d_y[v], 16)

            steps(pool, run)
        @block.vector
        def _(dve):
            ch = Chain(dve, cd)
            def stats(q):
                dve.wait_ge(l_x[q], 16)
                for t in range(q * QT, (q + 1) * QT):
                    ins = dve.bn_stats(st[:, t, :], X[:, t, :])
                ch.sync(ins)
                for t in range(q * QT, (q + 1) * QT):
                    ins = dve.bn_aggr(mv[:, t, :], st[:, t, :])
                ins.then_inc(s_var, 1)

            def invert(q):
                dve.wait_ge(s_std, q + 1)
                v = rstd[:, q * QT:(q + 1) * QT]
                dve.reciprocal(v, v).then_inc(s_rs, 1)

            def norm(g):
                dve.wait_ge(s_rs, g // 2 + 1)
                for t in norm_tiles(g, 0):
                    ins = dve.tensor_scalar(XR[:, t, 0:P], X[:, t, :], mv[:, t, 0:1], rstd[:, t:t + 1],
                                            ALU.subtract, ALU.mult)
                ins.then_inc(s_xn, 1)

            def pick(half, logits, mx, r, m):
                ch.sync(dve.tensor_reduce(sm[:, mx, half], logits[:, half], AX.X, ALU.max))
                ch.sync(dve.tensor_tensor(eq[:, half], logits[:, half], over_e(sm[:, mx, half]), ALU.is_equal))
                ch.sync(dve.tensor_tensor(eq[:, half], eq[:, half], rev_b, ALU.mult))
                ch.sync(dve.tensor_reduce(sm[:, r, half], eq[:, half], AX.X, ALU.max))
                ch.sync(dve.tensor_tensor(m[:, half], over_e(sm[:, r, half]), rev_b, ALU.is_equal))

            def choose(h):
                half = slice(h * HT, (h + 1) * HT)
                dve.wait_ge(l_gate, 32)
                dve.wait_ge(s_gl, (h + 1) * NG // 2)
                ch.sync(dve.tensor_tensor(lg[:, half], PS[:, G_BANK[h], 0:HT * NE].rearrange("p (t e) -> p t e", e=NE),
                                          gb[:].rearrange("p (a e) -> p a e", a=1).to_broadcast([P, HT, NE]), ALU.add))
                pick(half, lg, MX, R1, m1)
                dve.tensor_tensor(ex[:, half], lg[:, half], over_e(sm[:, MX, half]), ALU.subtract).then_inc(s_dl, 1)
                ch.sync(dve.scalar_tensor_tensor(out=lg2[:, half].rearrange("p t e -> p (t e)"),
                                                 in0=m1[:, half].rearrange("p t e -> p (t e)"), scalar=-BIG,
                                                 in1=lg[:, half].rearrange("p t e -> p (t e)"), op0=ALU.mult, op1=ALU.add))
                pick(half, lg2, MX2, R2, m2)
                ch.did(dve.tensor_tensor(mbf[:].rearrange("p e t -> p t e")[:, half], m1[:, half], m2[:, half], ALU.add))

            def weigh(h):
                half = slice(h * HT, (h + 1) * HT)
                dve.wait_ge(s_exg, h + 1)
                ch.did(dve.tensor_reduce(sm[:, SUM, half], ex[:, half], AX.X, ALU.add))
                ch.sync(dve.tensor_tensor(eq[:, half], ex[:, half], m2[:, half], ALU.mult))
                ch.did(dve.tensor_reduce(sm[:, CW2, half], eq[:, half], AX.X, ALU.add))
                ch.sync(dve.reciprocal(sm[:, CW1, half], sm[:, SUM, half]))
                dve.tensor_copy(XR[:, half, P + 1:P + 2], sm[:, CW1, half].rearrange("p (t a) -> p t a", a=1)).then_inc(s_cw, 1)
                dve.tensor_tensor(alt[:, half, 1:2], sm[:, CW2, half].rearrange("p (t a) -> p t a", a=1),
                                  sm[:, CW1, half].rearrange("p (t a) -> p t a", a=1), ALU.mult).then_inc(s_cw, 1)

            dve.memset(eps[:], EPS).then_inc(k_eps, 1)
            stats(0)
            invert(0)
            norm(0)
            norm(1)
            stats(1)
            invert(1)
            norm(2)
            stats(2)
            norm(3)
            invert(2)
            dve.wait_ge(l_ws, 16)
            dve.wait_ge(l_kc, 16)
            stats(3)
            dve.tensor_tensor(wbd[:], wqk[:], kc[:, K_BLK:K_BLK + P].rearrange("p (a b) -> p a b", a=1)
                              .to_broadcast([P, 3, P]), ALU.mult).then_inc(k_wbd, 1)
            dve.tensor_copy(lbf[:], kc[:, K_U:K_U + P])
            dve.tensor_copy(obf[:], kc[:, K_ONE:K_ONE + P]).then_inc(k_bf, 1)
            norm(4)
            norm(5)
            invert(3)
            norm(6)
            norm(7)
            choose(0)
            weigh(0)
            choose(1)
            ch.sync()
            dve.wait_ge(k_keep, 1)
            dve.tensor_tensor_scan(cum[:].rearrange("p e t -> p (e t)"), keep.rearrange("p e t -> p (e t)"),
                                   mbf[:].rearrange("p e t -> p (e t)"), 0.0, ALU.mult, ALU.add).then_inc(s_cum, 1)

            dve.wait_ge(s_tot, 1)
            ch.sync(dve.tensor_scalar(ntl[:], PS[:, 7, 0:NE], 127.0, None, ALU.add))
            ch.sync(dve.tensor_scalar(ntl[:], ntl[:], 7, None, ALU.arith_shift_right))
            ch.sync(dve.tensor_copy(se[:, TLF, :], ntl[:]))
            ch.sync(dve.tensor_tensor_scan(se[:, PIN, :], kc[:, K_ONE:K_ONE + NE], se[:, TLF, :], 0.0, ALU.mult, ALU.add))
            ch.sync(dve.tensor_tensor(se[:, BAS, :], se[:, PIN, :], se[:, TLF, :], ALU.subtract))
            ch.sync(dve.tensor_scalar(se[:, OFF, :], se[:, BAS, :], float(P), None, ALU.mult))
            dve.wait_ge(s_rk, 1)

            def place(h):
                half = slice(h * HT, (h + 1) * HT)
                ch.sync(dve.tensor_tensor(slot[:, half], PS[:, 4, :].rearrange("p (e t) -> p t e", e=NE)[:, half],
                                          se[:, OFF:OFF + 1, :].to_broadcast([P, HT, NE]), ALU.add))

            def index(k, h):
                half = slice(h * HT, (h + 1) * HT)
                m, r = ((m1, R1), (m2, R2))[k]
                ch.sync(dve.tensor_tensor(eq[:, half], slot[:, half], m[:, half], ALU.mult))
                ch.sync(dve.tensor_reduce(sm[:, r, half], eq[:, half], AX.X, ALU.add))
                dve.tensor_copy(idx[:, k, half], sm[:, r, half]).then_inc(s_idx, 1)

            for h in range(2):
                place(h)
                index(0, h)
            weigh(1)

            def gated(g, b):
                for c, (_, m) in enumerate(SCH):
                    if isinstance(g, int) and g < 2:
                        dve.wait_ge(s_si, g * NB + c + 1)
                    else:
                        dve.wait_ge(s_sg, 2 * (g * NB + c) + 2)
                    dve.tensor_tensor(sS[0:m, b, c, :], sS[0:m, b, c, :], sG[0:m, b, c, :], ALU.mult).then_inc(s_sm, 1)

            def add_z(g, b):
                dve.wait_ge(s_z, g + 1)
                v = X[:, bass.ds(g * GT, GT), :].rearrange("p t e -> p (t e)")
                dve.tensor_tensor(v, PS[:, 4 + b, :], v, ALU.add).then_inc(s_za, 1)

            def attend(part):
                for k in range(CT):
                    c = part * CT + k
                    prv = pr[:, bass.ds(c, 1), :].rearrange("p a (b h) -> p (a b) h", b=2).rearrange(
                        "p b (h a) -> p b h a", a=1).to_broadcast([P, 2, H, D])
                    vbv = Vb[:, bass.ds(c, 1), :].rearrange("p a (h e) -> p a h e", h=H).to_broadcast([P, 2, H, D])
                    ins = dve.tensor_tensor(at[:, k].rearrange("p b (h e) -> p b h e", h=H), prv, vbv, ALU.mult)
                ins.then_inc(s_at, 1)
                dve.wait_ge(s_at, part + 1)
                xv = X[:, bass.ds(part * CT * 2, CT * 2), :].rearrange("p t e -> p (t e)")
                dve.tensor_tensor(xv, xv, at[:].rearrange("p k b e -> p (k b e)"), ALU.add).then_inc(s_ax, 1)

            def score(g):
                dve.wait_ge(s_y, g + 1)
                dve.tensor_tensor(prod[:, g % 2, :].rearrange("p (t e) -> p t e", t=GT),
                                  PS[:, 6 + g % 2, :].rearrange("p (t e) -> p t e", t=GT),
                                  XR[:, g * GT:(g + 1) * GT, 0:P], ALU.mult).then_inc(s_pr, 1)
                dve.wait_ge(s_pr, g + 1)
                ch.did(dve.tensor_reduce(sc[:, g * GT * H:(g + 1) * GT * H],
                                         prod[:, g % 2, :].rearrange("p (r d) -> p r d", d=D), AX.X, ALU.add))

            gated(0, 0)
            score(0)
            score(1)
            gated(1, 1)
            for h in range(2):
                index(1, h)
            for g in range(2, NG):
                score(g)
            ch.sync()
            ch.sync(dve.tensor_tensor(
                ecmp, kc[0:1, K_TILE:K_TILE + NS].rearrange("p (s a) -> p s a", a=1).to_broadcast([1, NS, NE]),
                se[0:1, PIN:PIN + 1, :].to_broadcast([1, NS, NE]), ALU.is_ge))
            ch.sync(dve.tensor_reduce(emf[:], ecmp, AX.X, ALU.add))
            dve.tensor_scalar(emi[:], emf[:], float(NE - 1), None, ALU.min).then_inc(s_em, 1)
            for g in (0, 1):
                add_z(g, g)
            for g in (2, 3):
                gated(g, g % 2)
                for q in (2 * g - 4, 2 * g - 3):
                    dve.wait_ge(s_wh, q + 1)
                    cols = slice(q * WQ, (q + 1) * WQ)
                    dve.tensor_tensor(w13l[:, cols], w13[:, cols], w13h[:, cols].bitcast(F32), ALU.subtract).then_inc(s_wl, 1)
            ch.sync()
            sc_v = sc[:].rearrange("p (c r) -> p c r", c=C)
            mxa = se[:, 6:8, :].rearrange("p a e -> p (a e)")
            ch.sync(dve.tensor_reduce(mxa, sc_v.rearrange("p c r -> p r c"), AX.X, ALU.max))
            dve.tensor_tensor(sd[:], sc_v, mxa.rearrange("p (a r) -> p a r", a=1).to_broadcast([P, C, 2 * H]),
                              ALU.subtract).then_inc(s_ds, 1)
            for g in (2, 3):
                add_z(g, g % 2)
            dve.wait_ge(s_exa, 1)
            asum = se[:, 6:8, :].rearrange("p a e -> p (a e)")
            ch.sync(dve.tensor_reduce(asum, pr[:].rearrange("p c r -> p r c"), AX.X, ALU.add))
            ch.sync(dve.reciprocal(asum, asum))
            ch.sync(dve.tensor_tensor(pr[:], pr[:], asum.rearrange("p (a r) -> p a r", a=1).to_broadcast([P, C, 2 * H]), ALU.mult))
            dve.wait_ge(d_vb, 16)
            dve.wait_ge(s_za, 4)
            attend(0)
            dve.wait_ge(s_ax, 1)
            attend(1)
            dve.wait_ge(s_ax, 2)
            with dve.Fori(2, NG // 2) as it:
                for b in range(2):
                    gated(it * 2 + b, b)
                attend(it)
                dve.wait_ge(s_ax, it + 1)
                for b in range(2):
                    add_z(it * 2 + b, b)

            def run(j, u, fixed):
                if has(j + 1, fixed):
                    b = (u + 1) % 2
                    dve.wait_ge(r_xh, j + 2)
                    dve.tensor_tensor(rxl[:, b, :], PS[:, b, 0:P], rxh[:, b, :].bitcast(F32), ALU.subtract).then_inc(r_xl, 1)
                if has(j, fixed):
                    b = u % 2
                    dve.wait_ge(r_sg, j + 1)
                    dve.wait_ge(r_at, max(j - 1, 0) if fixed else j - 1)
                    dve.tensor_tensor(ra[:, b, :], sg[:, b, :], PS[:, 2 + b, F:F2], ALU.mult).then_inc(r_a, 1)
                if has(j - 2, fixed):
                    b, v = u % 2, (u - 2) % UN
                    dve.wait_ge(r_dn, j - 1)
                    dve.wait_ge(r_meta, j - 1)
                    if not fixed:
                        dve.wait_ge(d_y[v], j_turn(j, u, -2) * 16)
                    elif j - 2 >= UN:
                        dve.wait_ge(d_y[v], 16 * ((j - 2) // UN))
                    dve.tensor_scalar(yb[:, v, :], PS[:, 6 + b, 0:P], meta[:, v, 1:2], None, ALU.mult).then_inc(r_y, 1)

            steps(dve, run)
            def close(g, b, it, first):
                dve.wait_ge(d_yl[b], it * 16 + 16)
                if not first:
                    dve.wait_ge(d_o[b], it * 16)
                o = ob[:, b].rearrange("p (t e) -> p t e", t=CL)
                dve.tensor_tensor(o, yl[:, b, :, 0, :], X[:, bass.ds(g * CL, CL), :], ALU.add).then_inc(s_f1, 1)
                dve.wait_ge(s_f1, g + 1)
                dve.tensor_tensor(o, o, yl[:, b, :, 1, :], ALU.add).then_inc(s_f2, 1)

            for b in range(YL):
                close(b, b, 0, True)
            with dve.Fori(1, NC // YL) as it:
                for b in range(YL):
                    close(it * YL + b, b, it, False)

        @block.scalar
        def _(act):
            def deviation(q):
                act.wait_ge(s_var, q + 1)
                act.activation(rstd[:, q * QT:(q + 1) * QT], mv[:, q * QT:(q + 1) * QT, 1], ACT.Sqrt,
                               bias=eps[:, 0:1]).then_inc(s_std, 1)

            def early(n):
                g, c = n // NB, n % NB
                m = SCH[c][1]
                act.wait_ge(s_up, n + 1)
                act.activation(sS[0:m, g, c, :], PS[0:m, EARLY[n % 2][0], :], ACT.Identity, bias=sbc[0:m, c, 0:1]).then_inc(s_sg, 1)
                act.activation(sG[0:m, g, c, :], PS[0:m, EARLY[n % 2][1], :], ACT.Identity, bias=sbc[0:m, c, 1:2]).then_inc(s_sg, 1)

            def silus(g):
                for c, (_, m) in enumerate(SCH):
                    act.wait_ge(s_sg, 2 * (g * NB + c) + 2)
                    act.activation(sS[0:m, g, c, :], sS[0:m, g, c, :], ACT.Silu).then_inc(s_si, 1)

            def shifted_exp(h):
                act.wait_ge(s_dl, h + 1)
                v = ex[:, h * HT:(h + 1) * HT, :].rearrange("p t e -> p (t e)")
                act.activation(v, v, ACT.Exp).then_inc(s_exg, 1)

            act.wait_ge(k_eps, 1)
            act.activation(eps[:, 1:2], eps[:, 0:1], ACT.Sqrt)
            deviation(0)
            for g in range(NG):
                if g % 2 == 0 and g // 2 + 1 < NQ:
                    deviation(g // 2 + 1)
                act.wait_ge(s_tp, g + 1)
                for k in range(2):
                    act.activation(xnT[:, g * GW + k * T:g * GW + (k + 1) * T], PS[:, g % 2, k * T:(k + 1) * T],
                                   ACT.Copy, accum_out=xsum[:, 2 * g + k:2 * g + k + 1]).then_inc(s_xt, 1)
                if g == 2:
                    act.wait_ge(l_sh, 96)
                if g == NG - 2:
                    shifted_exp(0)

            def gates(g, b, c):
                m = SCH[c][1]
                k = (c + b) % 2
                act.wait_ge(s_up, g * NB + c + 1)
                act.activation(sS[0:m, b, c, :], PS[0:m, k, :], ACT.Silu, bias=sbc[0:m, c, 0:1]).then_inc(s_sg, 1)
                act.activation(sG[0:m, b, c, :], PS[0:m, 2 + k, :], ACT.Identity, bias=sbc[0:m, c, 1:2]).then_inc(s_sg, 1)

            for n in range(ER):
                early(n)
            act.wait_ge(k_mbd, 1)
            act.activation(mbd[:], PS[:, 0, 0:P], ACT.Copy).then_inc(k_mbd, 1)
            act.wait_ge(s_v, 1)
            act.activation(vS[:], PS[0:C, 1, 0:P], ACT.Copy).then_inc(s_vs, 1)
            shifted_exp(1)
            for n in range(ER, 2 * NB):
                early(n)
                if n == NB:
                    silus(0)
            silus(1)
            act.wait_ge(l_w13, 16)
            for q in range(NQ):
                act.activation(w13h[:, q * WQ:(q + 1) * WQ], w13[:, q * WQ:(q + 1) * WQ], ACT.Copy).then_inc(s_wh, 1)
            for g in (2, 3):
                act.wait_ge(s_z, g - 1)
                for c in range(NB):
                    gates(g, g % 2, c)
            act.wait_ge(s_ds, 1)
            act.activation(pr[:].rearrange("p c r -> p (c r)"), sd[:].rearrange("p c r -> p (c r)"), ACT.Exp,
                           scale=float(P) ** -0.5).then_inc(s_exa, 1)
            with act.Fori(2, NG // 2) as it:
                for b in range(2):
                    act.wait_ge(s_z, it * 2 + b - 1)
                    for c in range(NB):
                        gates(it * 2 + b, b, c)

            def run(j, u, fixed):
                if has(j + 1, fixed):
                    b = (u + 1) % 2
                    act.wait_ge(r_tp, j + 2)
                    act.wait_ge(r_up, max(j, 0) if fixed else j)
                    act.activation(rxh[:, b, :], PS[:, b, 0:P], ACT.Copy).then_inc(r_xh, 1)
                if has(j, fixed):
                    b = u % 2
                    act.wait_ge(r_up, j + 1)
                    act.wait_ge(r_a, max(j - 1, 0) if fixed else j - 1)
                    act.activation(sg[:, b, :], PS[:, 2 + b, 0:F], ACT.Silu).then_inc(r_sg, 1)
                if has(j - 1, fixed):
                    b = (u - 1) % 2
                    act.wait_ge(r_at, j)
                    act.wait_ge(r_dn, max(j - 2, 0) if fixed else j - 2)
                    act.activation(raT[:, b, :], PS[0:FH, 4 + b, 0:2 * P], ACT.Copy).then_inc(r_att, 1)

            steps(act, run)
            with act.Fori(0, NC // YL) as it:
                for b in range(YL):
                    g = it * YL + b
                    act.wait_ge(s_f2, g + 1)
                    act.dma_start(out_v[:, bass.ds(g * CL, CL), :], ob[:, b, :].rearrange("p (t e) -> p t e", t=CL)).then_inc(d_o[b], 16)

        @block.tensor
        def _(pe):
            pe.wait_ge(l_kc, 16)

            def turn(g):
                pe.wait_ge(s_xn, g + 1)
                if norm_tiles(g, 1):
                    pe.wait_ge(s_xp, g - 1)
                if g >= 2:
                    pe.wait_ge(s_xt, 2 * g - 2)
                for t in range(GT):
                    ins = pe.transpose(PS[:, g % 2, t * P:(t + 1) * P], XR[:, g * GT + t, 0:P], ident)
                ins.then_inc(s_tp, 1)

            def logits(g):
                pe.wait_ge(s_xt, 2 * g + 2)
                for t in range(g * GT, (g + 1) * GT):
                    k = t % HT
                    ins = pe.matmul(PS[:, G_BANK[t // HT], k * NE:(k + 1) * NE], xnT[:, t * P:(t + 1) * P], gw[:], start=True, stop=True)
                ins.then_inc(s_gl, 1)

            def project(g):
                if g >= 2:
                    pe.wait_ge(s_pr, g - 1)
                for t in range(GT):
                    tile = g * GT + t
                    ins = pe.matmul(PS[:, 6 + g % 2, t * P:(t + 1) * P], xnT[:, tile * P:(tile + 1) * P], mbd[:],
                                    start=True, stop=True)
                ins.then_inc(s_y, 1)

            def up(g, b, c, first):
                f, m = SCH[c]
                k = (c + b) % 2
                if not first:
                    pe.wait_ge(s_sg, 2 * (g * NB + c) - 2)
                xv = xnT[:, bass.ds(g * GW, GW)]
                pe.matmul(PS[0:m, k, :], sw1[:, f:f + m], xv, start=True, stop=True)
                pe.matmul(PS[0:m, 2 + k, :], sw3[:, f:f + m], xv, start=True, stop=True).then_inc(s_up, 1)

            def early(n):
                f, m = SCH[n % NB]
                if n >= 2:
                    pe.wait_ge(s_sg, 2 * n - 2)
                xv = xnT[:, (n // NB) * GW:(n // NB + 1) * GW]
                pe.matmul(PS[0:m, EARLY[n % 2][0], :], sw1[:, f:f + m], xv, start=True, stop=True)
                pe.matmul(PS[0:m, EARLY[n % 2][1], :], sw3[:, f:f + m], xv, start=True, stop=True).then_inc(s_up, 1)

            def down(g, b, first):
                pe.wait_ge(s_sm, g * NB + NB)
                if not first:
                    pe.wait_ge(s_za, g - 1)
                for t in range(GT):
                    zt = PS[:, 4 + b, t * P:(t + 1) * P]
                    pe.matmul(zt, obf[0:3, :], bsh[:], start=True, stop=False)
                    for c, (_, m) in enumerate(SCH):
                        ins = pe.matmul(zt, sS[0:m, b, c, t * P:(t + 1) * P], sw2[0:m, c, :], start=False, stop=(c == NB - 1))
                ins.then_inc(s_z, 1)

            turn(0)
            turn(1)
            pe.wait_ge(l_gate, 32)
            for g in range(NG):
                logits(g)
                if g + 2 < NG:
                    turn(g + 2)
                if g == EG:
                    pe.wait_ge(l_sh, 96)
                if g >= EG:
                    early(g - EG)
            for n in range(NG - EG, ER):
                early(n)
            pe.wait_ge(k_wbd, 1)
            pe.wait_ge(s_xt, 2 * NG)
            pe.matmul(PS[:, 0, 0:P], wbd[:, 0, :], wbd[:, 1, :], start=True, stop=True).then_inc(k_mbd, 1)
            pe.matmul(PS[0:C, 1, 0:P], xsum[:], wbd[:, 2, :], start=True, stop=True).then_inc(s_v, 1)
            pe.wait_ge(k_bf, 1)
            pe.wait_ge(s_cum, 1)
            pe.matmul(PS[:, 7, 0:NE], obf[:], cum[:, :, NT - 1], start=True, stop=True).then_inc(s_tot, 1)
            pe.matmul(PS[:, 4, :], lbf[:], mbf[:].rearrange("p e t -> p (e t)"), start=True, stop=False)
            pe.matmul(PS[:, 4, :], obf[:], cum[:].rearrange("p e t -> p (e t)"), start=False, stop=True).then_inc(s_rk, 1)
            for n in range(ER, 2 * NB):
                early(n)
            pe.wait_ge(k_mbd, 2)
            pe.wait_ge(s_sg, 4 * NB)
            project(0)
            pe.wait_ge(s_idx, 1)
            project(1)
            pe.wait_ge(d_bld, 16)
            down(0, 0, True)
            project(2)
            project(3)
            down(1, 1, True)
            for g in range(4, NG):
                project(g)
            for g in (2, 3):
                for c in range(NB):
                    up(g, g % 2, c, False)
            down(2, 0, False)
            down(3, 1, False)
            with pe.Fori(2, NG // 2) as it:
                for b in range(2):
                    for c in range(NB):
                        up(it * 2 + b, b, c, False)
                for b in range(2):
                    down(it * 2 + b, b, False)

            pe.wait_ge(s_wl, NQ)
            pe.wait_ge(l_w2, 16)
            pe.wait_ge(s_em, 1)
            pe.wait_ge(s_sg, 2 * NG * NB)

            held = [pe.alloc_register(f"expert{v}") for v in range(UN)]

            def read_expert(j, u):
                at = slice(j, j + 1) if isinstance(j, int) else bass.ds(j, 1)
                pe.reg_load(held[u % UN], emi[0:1, at])

            def expert(u):
                return pe.snap(held[u % UN], min_val=0, max_val=NE - 1)

            def run(j, u, fixed):
                if has(j + 1, fixed):
                    b, v = (u + 1) % 2, (u + 1) % UN
                    pe.wait_ge(d_rx[v], 16 * ((j + 1) // UN + 1) if fixed else j_turn(j, u, 1) * 16 + 16)
                    pe.transpose(PS[:, b, 0:P], RX[:, v, 0:P], ident).then_inc(r_tp, 1)
                if has(j, fixed):
                    b = u % 2
                    e = expert(u)
                    pe.wait_ge(r_xl, j + 1)
                    for k, (x, w) in enumerate(((rxh, w13h), (rxl, w13h), (rxh, w13l))):
                        pe.matmul(PS[:, 2 + b, 0:F2], x[:, b, :], w[:, bass.ds(e * F2, F2)], start=(k == 0), stop=False)
                    pe.matmul(PS[:, 2 + b, 0:F2], obf[0:3, :], bsp[:, bass.ds(e * F2, F2)], start=False,
                              stop=True).then_inc(r_up, 1)
                    if has(j + 1, fixed):
                        read_expert(j + 1, u + 1)
                if has(j - 1, fixed):
                    b = (u - 1) % 2
                    pe.wait_ge(r_a, j)
                    if fixed and j == 1:
                        pe.wait_ge(s_za, NG)
                    pe.transpose(PS[0:FH, 4 + b, 0:P], ra[:, b, 0:FH], ident)
                    pe.transpose(PS[0:FH, 4 + b, P:2 * P], ra[:, b, FH:F], ident).then_inc(r_at, 1)
                if has(j - 2, fixed):
                    b = u % 2
                    e = expert(u - 2)
                    pe.wait_ge(r_att, j - 1)
                    if not has(j - 1, fixed):
                        pe.wait_ge(r_y, j - 3)
                    for k in range(2):
                        pe.matmul(PS[:, 6 + b, 0:P], raT[:, b, k * P:(k + 1) * P],
                                  w2[:, bass.ds(e * 2 * P + k * P, P)], start=(k == 0), stop=False)
                    pe.matmul(PS[:, 6 + b, 0:P], obf[0:3, :], bsp[:, bass.ds(e * P + NE * F2, P)], start=False,
                              stop=True).then_inc(r_dn, 1)

            pe.wait_ge(d_bld, 32)
            read_expert(0, 0)
            steps(pe, run)


def constants():
    import numpy as np
    k = np.zeros((P, KW), np.float32)
    i, j = np.arange(P)[:, None], np.arange(P)[None, :]
    k[:, K_ID:K_ID + P] = i == j
    k[:, K_BLK:K_BLK + P] = i // D == j // D
    k[:, K_U:K_U + P] = -1.0 * (i >= j)
    k[:, K_ONE:K_ONE + P] = 1
    k[:, K_REV:K_REV + NE] = NE - np.arange(NE)
    k[:, K_TILE:K_TILE + NS] = np.arange(NS)
    kb = k.view(np.int32)
    kb[:, K_TOK:K_TOK + NT] = (i * NT + np.arange(NT)[None, :]) * 2
    kb[:, K_TOK2:K_TOK2 + NT] = kb[:, K_TOK:K_TOK + NT] + 1
    kb[:, K_PAD:K_PAD + NS] = 2 * N + i * NS + np.arange(NS)[None, :]
    return k


def arrays_of(inp):
    import numpy as np
    a = {n: np.asarray(v) for n, v in inp.items()}
    f = "L0_ffn_"
    w13 = np.concatenate([a[f + "w1"], a[f + "w3"]], axis=2)
    b13 = np.concatenate([a[f + "b1"], a[f + "b3"]], axis=1)
    r = {
        "x": a["L0_attn_x"].reshape(N, P),
        "kc": constants(),
        "wqk": np.concatenate([np.tile(a["L0_attn_Wq"], (H, H)), np.tile(a["L0_attn_Wk"], (H, H)),
                               np.tile(a["L0_attn_Wv"].T, (H, H))], axis=1),
        "gate_w": a[f + "gate_w"], "gate_b": a[f + "gate_b"].reshape(1, NE),
        "biases": np.concatenate([b13.reshape(-1), a[f + "b2"].reshape(-1), a[f + "sb2"]]).reshape(P, NBIAS // P),
        "sw1": a[f + "sw1"], "sw3": a[f + "sw3"], "sw2": a[f + "sw2"],
        "sb_a": np.stack([a[f + "sb1"][:256].reshape(2, P).T, a[f + "sb3"][:256].reshape(2, P).T], axis=2),
        "sb_b": np.stack([a[f + "sb1"][256:], a[f + "sb3"][256:]], axis=1)[:, None, :],
        "w13": w13.transpose(1, 0, 2).reshape(P, NE * F2),
        "w2": a[f + "w2"].reshape(NE, 2, FH, P).transpose(2, 0, 1, 3).reshape(FH, NE * 2 * P),
    }
    return {n: np.ascontiguousarray(v) for n, v in r.items()}


def program(nc, arrays):
    d = {n: nc.dram_tensor(f"in_{n}", v.shape, mybir.dt.from_np(v.dtype), kind="ExternalInput").ap()
         for n, v in arrays.items()}
    d["out"] = nc.dram_tensor("out_0", (N, P), F32, kind="ExternalOutput").ap()
    build(nc, d)


def kernel(**inputs):
    import concourse.bacc as bacc
    from concourse.bass_utils import run_bass_kernel_spmd
    arrays = arrays_of(inputs)
    nc = bacc.Bacc("TRN2", target_bir_lowering=False, num_devices=1)
    program(nc, arrays)
    r = run_bass_kernel_spmd(nc, [{f"in_{n}": v for n, v in arrays.items()}], core_ids=[0])
    return r.results[0]["out_0"].reshape(C, T, P)
```
